# Optimizing a Trainium2 kernel written in Bass

```python
import numpy as np
import jax
import jax.numpy as jnp

def _softmax(x, axis=-1):
    return jax.nn.softmax(x, axis=axis)

def _gelu(x):
    return jax.nn.gelu(x, approximate=True)

def _silu(x):
    return jax.nn.silu(x)

def _sigmoid(x):
    return jax.nn.sigmoid(x)

def _layernorm(x, axis=-1, eps=1e-05):
    m = jnp.mean(x, axis=axis, keepdims=True)
    v = jnp.var(x, axis=axis, keepdims=True)
    return (x - m) / jnp.sqrt(v + eps)

def _scatter_add(tgt, idx, src, axis=0):
    return tgt.at[idx].add(src)

def _segment_sum(src, seg, n):
    return jax.ops.segment_sum(src, seg, n)
kernel_name = 'mk_metaformer_d1_conv_nchw128_r4_de9199'

def setup_inputs(seed: int=0):
    np.random.seed(seed)
    _w = jnp.asarray

    def _rec_inputs():
        import jax
        import jax.numpy as jnp
        _gk = jax.random.key(seed)
        x = -7.109e-05 + 0.9999 * jax.random.normal(jax.random.fold_in(_gk, 1), (8, 32, 64, 64), jnp.float32)
        return x
    x = _rec_inputs()

    def _L0_conv_setup():
        import jax, jax.numpy as jnp
        import numpy as np
        HEADS = 4
        DIM_HEAD = 32
        LN_EPS = 1e-05
        key = jax.random.key(seed)
        k1, k2, k3 = jax.random.split(key, 3)
        B, C, T, F = (8, 32, 64, 64)
        hidden = HEADS * DIM_HEAD
        x = jax.random.normal(k1, (B, C, T, F), dtype=jnp.float32)
        w_qkv = jax.random.normal(k2, (hidden * 3, C), dtype=jnp.float32) * (1.0 / np.sqrt(C))
        b_qkv = jnp.zeros((hidden * 3,), dtype=jnp.float32)
        w_out = jax.random.normal(k3, (C, hidden), dtype=jnp.float32) * (1.0 / np.sqrt(hidden))
        b_out = jnp.zeros((C,), dtype=jnp.float32)
        g_ln = jnp.ones((C,), dtype=jnp.float32)
        return {'x': x, 'w_qkv': w_qkv, 'b_qkv': b_qkv, 'w_out': w_out, 'b_out': b_out, 'g_ln': g_ln}
    _L0_conv_all = _L0_conv_setup()
    _L0_conv_in = {k: v for k, v in _L0_conv_all.items() if k in ('w_qkv', 'b_qkv', 'w_out', 'b_out', 'g_ln')}
    del _L0_conv_all

    def _L0_ffn_setup():
        import jax, jax.numpy as jnp
        import numpy as np
        B, N, D, C, E, K = (8, 2048, 32, 32, 8, 2)
        key = jax.random.key(seed)
        k0, k1, k2 = jax.random.split(key, 3)
        x = jax.random.normal(k0, (B, N, D), dtype=jnp.float32)
        router_w = jax.random.normal(k1, (D, E), dtype=jnp.float32) * 0.05
        router_b = jnp.zeros((E,), dtype=jnp.float32)
        expert_w = jax.random.normal(k2, (E, D, C), dtype=jnp.float32) * (1.0 / np.sqrt(D))
        expert_b = jnp.zeros((E, C), dtype=jnp.float32)
        return {'x': x, 'router_w': router_w, 'router_b': router_b, 'expert_w': expert_w, 'expert_b': expert_b}
    _L0_ffn_all = _L0_ffn_setup()
    _L0_ffn_in = {k: v for k, v in _L0_ffn_all.items() if k in ('router_w', 'router_b', 'expert_w', 'expert_b')}
    del _L0_ffn_all
    return {'x': x, 'L0_conv_w_qkv': _L0_conv_in['w_qkv'], 'L0_conv_b_qkv': _L0_conv_in['b_qkv'], 'L0_conv_w_out': _L0_conv_in['w_out'], 'L0_conv_b_out': _L0_conv_in['b_out'], 'L0_conv_g_ln': _L0_conv_in['g_ln'], 'L0_ffn_router_w': _L0_ffn_in['router_w'], 'L0_ffn_router_b': _L0_ffn_in['router_b'], 'L0_ffn_expert_w': _L0_ffn_in['expert_w'], 'L0_ffn_expert_b': _L0_ffn_in['expert_b']}

def reference(x, L0_conv_w_qkv, L0_conv_b_qkv, L0_conv_w_out, L0_conv_b_out, L0_conv_g_ln, L0_ffn_router_w, L0_ffn_router_b, L0_ffn_expert_w, L0_ffn_expert_b):
    import jax
    import jax.numpy as jnp

    def _L0_conv_ref(x, w_qkv, b_qkv, w_out, b_out, g_ln):
        import jax, jax.numpy as jnp
        import numpy as np
        HEADS = 4
        DIM_HEAD = 32
        LN_EPS = 1e-05
        b, c, t, f = x.shape
        n = t * f
        scale = DIM_HEAD ** (-0.5)
        qkv = jnp.einsum('bcxy,oc->boxy', x, w_qkv) + b_qkv[None, :, None, None]
        q, k, v = jnp.split(qkv, 3, axis=1)
        q = q.reshape(b, HEADS, DIM_HEAD, n)
        k = k.reshape(b, HEADS, DIM_HEAD, n)
        v = v.reshape(b, HEADS, DIM_HEAD, n)
        q = jax.nn.softmax(q, axis=-2) * scale
        k = jax.nn.softmax(k, axis=-1)
        v = v / n
        context = jnp.einsum('bhdn,bhen->bhde', k, v)
        out = jnp.einsum('bhde,bhdn->bhen', context, q)
        out = out.reshape(b, HEADS * DIM_HEAD, t, f)
        out = jnp.einsum('bcxy,oc->boxy', out, w_out) + b_out[None, :, None, None]
        mean = out.mean(axis=1, keepdims=True)
        var = out.var(axis=1, keepdims=True)
        out = (out - mean) * jax.lax.rsqrt(var + LN_EPS) * g_ln[None, :, None, None]
        return out

    def _L0_ffn_ref(x, router_w, router_b, expert_w, expert_b):
        import jax, jax.numpy as jnp
        import numpy as np
        B, N, D, C, E, K = (8, 2048, 32, 32, 8, 2)
        router_probs = jax.nn.softmax(x @ router_w + router_b, axis=-1)
        top_p, top_i = jax.lax.top_k(router_probs, K)
        top_p = top_p / jnp.sum(top_p, axis=-1, keepdims=True)
        expert_out = jnp.einsum('bnd,edc->bnec', x, expert_w) + expert_b
        gathered = jnp.take_along_axis(expert_out, top_i[..., None], axis=2)
        return jnp.einsum('bnk,bnkc->bnc', top_p, gathered)

    def _gn(v, G=32, eps=1e-05):
        B_, C_, H_, W_ = v.shape
        g = v.reshape(B_, G, C_ // G, H_, W_)
        m = jnp.mean(g, axis=(2, 3, 4), keepdims=True)
        s = jnp.var(g, axis=(2, 3, 4), keepdims=True)
        return ((g - m) / jnp.sqrt(s + eps)).reshape(v.shape)

    def _ln_c(v, eps=1e-06):
        m = jnp.mean(v, axis=1, keepdims=True)
        s = jnp.var(v, axis=1, keepdims=True)
        return (v - m) / jnp.sqrt(s + eps)

    def _ln_t(v, eps=1e-05):
        m = jnp.mean(v, axis=-1, keepdims=True)
        s = jnp.var(v, axis=-1, keepdims=True)
        return (v - m) / jnp.sqrt(s + eps)

    def _to_tokens(v):
        B_, C_, H_, W_ = v.shape
        return v.reshape(B_, C_, H_ * W_).transpose(0, 2, 1)

    def _from_tokens(t, like):
        B_, C_, H_, W_ = like.shape
        return t.transpose(0, 2, 1).reshape(B_, C_, H_, W_)
    x = x + _L0_conv_ref(_ln_c(x), L0_conv_w_qkv, L0_conv_b_qkv, L0_conv_w_out, L0_conv_b_out, L0_conv_g_ln)
    t = _to_tokens(x)
    t = t + _L0_ffn_ref(_ln_t(t), L0_ffn_router_w, L0_ffn_router_b, L0_ffn_expert_w, L0_ffn_expert_b)
    x = _from_tokens(t, x)
    return x

_drawn_inputs = setup_inputs


def setup_inputs(seed=0):
    import zlib

    import numpy as np

    out = dict(_drawn_inputs(seed))
    spreads = {'L0_conv_b_qkv': (0.0, 2.0),
     'L0_conv_b_out': (0.0, 0.1),
     'L0_conv_g_ln': (1.0, 0.2),
     'L0_ffn_router_b': (0.0, 0.1),
     'L0_ffn_expert_b': (0.0, 0.1)}
    factors = {'L0_conv_w_qkv': 8.0, 'L0_conv_w_out': 8.0}
    for name, (base, spread) in spreads.items():
        noise = np.random.default_rng([zlib.crc32(name.encode()), seed]).standard_normal(out[name].shape)
        drawn = base * np.exp(spread * noise) if base else spread * noise
        out[name] = jnp.asarray(drawn.astype(out[name].dtype))
    for name, factor in factors.items():
        out[name] = (out[name] * factor).astype(out[name].dtype)
    return out
```

```python
import concourse.bass as bass
from concourse import mybir
from contextlib import ExitStack

NB, C, N = 8, 32, 4096
HEADS, DH = 4, 32
CH = HEADS * DH
P = 128
G = N // P
J = P // C
T = G // J
E = 8
EPS = 1e-5
EPS_IN = 1e-6
SCALE = DH ** -0.5

QMAX, NORM, KMAX, GATE = 4, 8, 4, 8
QEXP, XT, STACK, KEXP, OUTU = 8, 2, 4, 8, 2
SETUP_V = 29


def build(nc, x, w_qkv, b_qkv, w_out, b_out, g_ln, router_w, router_b, expert_w, expert_b, out):
    f32, f16, u32 = mybir.dt.float32, mybir.dt.float16, mybir.dt.uint32
    ALU, ACT, AX = mybir.AluOpType, mybir.ActivationFunctionType, mybir.AxisListType
    x_v = x.rearrange("b c (j t) f -> b j c (t f)", j=J)
    out_v = out.rearrange("b c (j t) f -> b j c (t f)", j=J)

    ctx = ExitStack()
    with ctx:
        def sb(name, shape, dt=f32):
            return ctx.enter_context(nc.sbuf_tensor(name, shape, dt))

        def sem(name):
            return ctx.enter_context(nc.semaphore(name))

        ident = sb("ident", [P, P])
        ident16 = sb("ident16", [P, P], f16)
        ones = sb("ones", [P, P])
        headmask = sb("headmask", [P, HEADS, C])
        ctxscale = sb("ctxscale", [P, HEADS, C])
        ctxbias = sb("ctxbias", [P, HEADS, C])
        bout_rep = sb("bout_rep", [P, C])
        g_rep = sb("g_rep", [P, C])
        maxpick = sb("maxpick", [P, 16, CH], f16)
        rank = sb("rank", [P, G, E])
        row_high = sb("row_high", [P, 1])
        row_low = sb("row_low", [P, 1])
        w_nat = sb("w_nat", [P, 3, C])
        b_nat = sb("b_nat", [P, 3])
        qk_nat = sb("qk_nat", [P, 2, P])
        v_nat = sb("v_nat", [P, C + 1])
        wo_nat = sb("wo_nat", [C, P])
        wo_block = sb("wo_block", [P, HEADS, C])
        u_mat = sb("u_mat", [C + 1, P])
        NW = 2 * CH + E * C + E
        w_rows = sb("w_rows", [P, NW])
        w_high = sb("w_high", [P, NW], f16)
        w_low = sb("w_low", [P, NW], f16)
        w_stack = sb("w_stack", [P, NW], f16)
        groups = [(0, 2 * CH), (2 * CH, 2 * CH + E * C), (2 * CH + E * C, NW)]
        amax = sb("amax", [P, 3])
        gmax = sb("gmax", [3, 1])
        gpow = sb("gpow", [3, 1])
        gdiag = sb("gdiag", [3, 3])
        wscale = sb("wscale", [P, 3])
        winv = sb("winv", [P, 3])
        ws_q = w_stack[:, 0:CH]
        ws_k = w_stack[:, CH:2 * CH]
        ws_e = w_stack[:, 2 * CH:2 * CH + E * C]
        ws_r = w_stack[:, 2 * CH + E * C:NW]
        x_in = sb("x_in", [P, N // J])
        x_tok = sb("x_tok", [P, 2, G * C])
        LN = (1, 2, 3)
        centered = {k: sb(f"centered{k}", [P, G * C]) for k in LN}
        squares = {k: sb(f"squares{k}", [P, G * C]) for k in LN}
        nsum = {k: sb(f"nsum{k}", [P, G]) for k in LN}
        nmean = {k: sb(f"nmean{k}", [P, G]) for k in LN}
        vsum = {k: sb(f"vsum{k}", [P, G]) for k in LN}
        vari = {k: sb(f"vari{k}", [P, G]) for k in LN}
        lnv = {k: sb(f"lnv{k}", [P, G]) for k in LN}
        r0 = {k: sb(f"r0_{k}", [P, G]) for k in LN}
        rr = {k: sb(f"rr{k}", [P, G]) for k in LN}
        ru = {k: sb(f"ru{k}", [P, G]) for k in LN}
        rstd = {k: sb(f"rstd{k}", [P, G]) for k in LN}
        xhat = sb("xhat", [P, G, C + 1])
        xhat3 = sb("xhat3", [P, G, C])
        parts = {k: sb(f"parts{k}", [P, G, P], f16) for k in (1, 3)}
        stack = {k: sb(f"stack{k}", [P, N], f16) for k in (1, 3)}
        kmax = sb("kmax", [P, KMAX])
        nkmax = sb("nkmax", [P, 1])
        kmax_nat = sb("kmax_nat", [P, P], f16)
        ws_kmax = sb("ws_kmax", [P, CH], f16)
        ek = sb("ek", [P, 2, 4, CH])
        gnat = sb("gnat", [P, P])
        grec = sb("grec", [P, 1])
        gtr = sb("gtr", [C + 1, P])
        mix = sb("mix", [P, P])
        mixz = sb("mixz", [P, P + HEADS])
        nqmax = sb("nqmax", [P, 2, 16 * HEADS])
        qmax_nat = sb("qmax_nat", [P, 2, 2, 16 * HEADS], f16)
        qmax_tr = sb("qmax_tr", [P, 2, P], f16)
        eq = sb("eq", [P, 2, 4 * P])
        zrec = sb("zrec", [P, 2, 4, HEADS])
        heads = sb("heads", [P, G, CH])
        pairs = sb("pairs", [P, G, 2 * C])
        attn = sb("attn", [P, G * C])
        scaled = sb("scaled", [P, G * C])
        gained = sb("gained", [P, G * C])
        x2 = sb("x2", [P, G * C])
        logit = sb("logit", [P, G, E])
        logit2 = sb("logit2", [P, G, E])
        tie1 = sb("tie1", [P, G, E])
        tie2 = sb("tie2", [P, G, E])
        one1 = sb("one1", [P, G, E])
        one2 = sb("one2", [P, G, E])
        gates = sb("gates", [P, G, E])
        top1 = sb("top1", [P, G])
        top2 = sb("top2", [P, G])
        pick1 = sb("pick1", [P, G])
        pick2 = sb("pick2", [P, G])
        gap = sb("gap", [P, G])
        e2 = sb("e2", [P, G])
        den = sb("den", [P, G])
        g1 = sb("g1", [P, G])
        g2 = sb("g2", [P, G])
        gated = sb("gated", [P, 2, E, 4, C])
        y_out = sb("y_out", [P, N // J])

        wide = ctx.enter_context(nc.psum_tensor("wide", [P, 2, 1024], f32))
        narrow = ctx.enter_context(nc.psum_tensor("narrow", [P, 2, 512], f32))
        ctxsum = ctx.enter_context(nc.psum_tensor("ctxsum", [P, 512], f32))
        small = ctx.enter_context(nc.psum_tensor("small", [P, 512], f32))

        loaded = sem("weights_loaded")
        made = sem("constants_made")
        setup_v = sem("setup_vector_steps")
        setup_t = sem("setup_tensor_steps")
        x_loaded = sem("x_loaded")
        stored = sem("stored")
        wide_full, wide_free = sem("wide_full"), sem("wide_free")
        narrow_full, narrow_free = sem("narrow_full"), sem("narrow_free")
        small_full, small_free = sem("small_full"), sem("small_free")
        ctx_free = sem("ctx_free")
        mean_ready = {k: sem(f"mean_ready{k}") for k in LN}
        center_ready = {k: sem(f"center_ready{k}") for k in LN}
        square_ready = {k: sem(f"square_ready{k}") for k in LN}
        var_ready = {k: sem(f"var_ready{k}") for k in LN}
        r0_ready = {k: sem(f"r0_ready{k}") for k in LN}
        rstd_ready = {k: sem(f"rstd_ready{k}") for k in LN}
        xhat_ready = {k: sem(f"xhat_ready{k}") for k in LN}
        parts_ready = {k: sem(f"parts_ready{k}") for k in (1, 3)}
        kmax_nat_ready = sem("kmax_nat_ready")
        ek_used = sem("ek_used")
        mixz_ready = sem("mixz_ready")
        qmax_nat_ready = sem("qmax_nat_ready")
        attn_ready = sem("attn_ready")
        x2_ready = sem("x2_ready")
        gap_ready, e2_ready = sem("gap_ready"), sem("e2_ready")
        gated_used = sem("gated_used")
        y_ready = sem("y_ready")
        front_v, back_v = sem("front_vector_steps"), sem("back_vector_steps")
        back_a = sem("back_scalar_steps")
        front_a = sem("front_scalar_steps")
        back_p = sem("back_pool_steps")
        FRONT_V, BACK_V = 8, 37

        class Chain:

            def __init__(self, eng, s, base):
                self.eng, self.s, self.base, self.n = eng, s, base, 0

            def inc(self, ins):
                ins.then_inc(self.s, 1)
                self.n += 1
                return self

            def wait(self):
                self.eng.wait_ge(self.s, self.base + self.n)

        class Places:

            def __init__(self, i, front, back):
                self.w = 24 * i - 20 if back else 0
                self.n = 28 * i - 14 if back else 0
                self.s = 6 * i - 3 if back else 0
                w = n = s = 0
                if front:
                    self.xt, n = n, n + XT
                if back:
                    self.qmax, w = w, w + QMAX
                    self.qtr, s = s, s + 2
                    self.qexp, n = n, n + QEXP
                    self.norm, w = w, w + NORM
                if front:
                    self.stack1, n = n, n + STACK
                    self.kmax, w = w, w + KMAX
                    self.ktr, s = s, s + 1
                    self.kexp, n = n, n + KEXP
                    self.gtr, s = s, s + 1
                    self.mix, s = s, s + 1
                if back:
                    self.stack3, n = n, n + STACK
                    self.logit, s = s, s + 1
                    self.gate, w = w, w + GATE
                    self.out, n = n, n + OUTU

        def run(engine, iteration):
            iteration(0, True, False)
            with engine.Fori(1, NB) as i:
                iteration(i, True, True)
            iteration(NB, False, True)

        def wait_slot(eng, free, at, slots):
            if isinstance(at, int) and at < slots:
                return
            eng.wait_ge(free, at - slots + 1)

        block = ctx.enter_context(nc.Block())

        @block.sync
        def _(sp):
            def load(b):
                sp.dma_start(x_in[:, :], x_v[bass.ds(b, 1)].rearrange("b j c i -> (b j) c i")).then_inc(x_loaded, 16)

            load(0)
            sp.dma_start(w_nat[:, :, :], w_qkv.rearrange("(s p) c -> p s c", p=P)).then_inc(loaded, 16)
            sp.dma_start(b_nat[:, :], b_qkv.rearrange("(s p) -> p s", p=P),
                         allow_slow_non_contiguous=True).then_inc(loaded, 16)
            sp.dma_start(wo_nat[:, :], w_out).then_inc(loaded, 16)
            sp.dma_start(bout_rep[:, :], b_out.partition_broadcast(P)).then_inc(loaded, 16)
            sp.dma_start(g_rep[:, :], g_ln.partition_broadcast(P)).then_inc(loaded, 16)
            sp.wait_ge(made, 1)
            lo, hi = groups[1]
            for r in range(3):
                rows = slice(C * r, C * r + C)
                sp.dma_start(w_rows[rows, lo:hi].rearrange("d (e c) -> d e c", e=E),
                             expert_w.rearrange("e d c -> d e c")).then_inc(loaded, 16)
                sp.dma_start(w_rows[rows, hi:NW], router_w).then_inc(loaded, 16)
            for r in (96, 97):
                sp.dma_start(w_rows[r:r + 1, lo:hi],
                             expert_b.rearrange("e c -> (e c)").unsqueeze(0)).then_inc(loaded, 16)
                sp.dma_start(w_rows[r:r + 1, hi:NW], router_b.unsqueeze(0)).then_inc(loaded, 16)

            def store(b):
                sp.wait_ge(y_ready, OUTU * b + OUTU)
                sp.dma_start(out_v[bass.ds(b, 1)].rearrange("b j c i -> (b j) c i"), y_out[:, :]).then_inc(stored, 16)

            def iteration(i, front, back):
                if back and front:
                    sp.wait_ge(mean_ready[1], i)
                    load(i)
                if back:
                    store(i - 1)

            run(sp, iteration)
            sp.wait_ge(stored, 16 * NB)

        @block.gpsimd
        def _(pool):
            nc.gpsimd.memset(w_rows[:], 0.0).then_inc(made, 1)
            nc.gpsimd.memset(ones[:], 1.0).then_inc(made, 1)
            nc.gpsimd.memset(maxpick[:], 0.0).then_inc(made, 1)
            nc.gpsimd.memset(qk_nat[:], 0.0).then_inc(made, 1)
            nc.gpsimd.memset(kmax_nat[:], 0.0).then_inc(made, 1)
            nc.gpsimd.memset(gnat[:], 0.0).then_inc(made, 1)
            nc.gpsimd.memset(xhat[:, :, C:C + 1], 1.0).then_inc(made, 1)
            for k in (1, 3):
                nc.gpsimd.memset(parts[k][:, :, 96:P], 1.0).then_inc(made, 1)
            pool.wait_ge(made, 9)
            nc.gpsimd.affine_select(out=ident[:], in_=ones[:], pattern=[[-1, P]], compare_op=ALU.is_equal,
                                    fill=0.0, base=0, channel_multiplier=1).then_inc(made, 1)
            nc.gpsimd.affine_select(out=ident16[:], in_=ones[:], pattern=[[-1, P]], compare_op=ALU.is_equal,
                                    fill=0.0, base=0, channel_multiplier=1).then_inc(made, 1)
            nc.gpsimd.affine_select(out=headmask[:], in_=ones[:].rearrange("p (h c) -> p h c", h=HEADS),
                                    pattern=[[-DH, HEADS], [0, C]], compare_op=ALU.is_ge,
                                    fill=0.0, base=0, channel_multiplier=1).then_inc(made, 1)
            nc.gpsimd.affine_select(out=maxpick[:].rearrange("p t (h d) -> p t h d", h=HEADS),
                                    in_=maxpick[:].rearrange("p t (h d) -> p t h d", h=HEADS),
                                    pattern=[[-HEADS, 16], [-1, HEADS], [0, DH]], compare_op=ALU.not_equal,
                                    fill=1.0, base=0, channel_multiplier=1).then_inc(made, 1)
            nc.gpsimd.affine_select(out=row_high[:], in_=ones[:, 0:1], pattern=[[0, 1]], compare_op=ALU.is_ge,
                                    fill=0.0, base=63, channel_multiplier=-1).then_inc(made, 1)
            nc.gpsimd.affine_select(out=row_low[:], in_=ones[:, 0:1], pattern=[[0, 1]], compare_op=ALU.is_ge,
                                    fill=0.0, base=-64, channel_multiplier=1).then_inc(made, 1)
            pool.wait_ge(made, 15)
            nc.gpsimd.affine_select(out=headmask[:], in_=headmask[:], pattern=[[DH, HEADS], [0, C]],
                                    compare_op=ALU.is_ge, fill=0.0, base=DH - 1,
                                    channel_multiplier=-1).then_inc(made, 1)
            nc.gpsimd.affine_select(out=maxpick[:].rearrange("p t (h d) -> p t h d", h=HEADS),
                                    in_=maxpick[:].rearrange("p t (h d) -> p t h d", h=HEADS),
                                    pattern=[[-HEADS, 16], [-1, HEADS], [0, DH]], compare_op=ALU.not_equal,
                                    fill=1.0, base=-64, channel_multiplier=1).then_inc(made, 1)
            nc.gpsimd.affine_select(out=row_high[:], in_=row_high[:], pattern=[[0, 1]], compare_op=ALU.not_equal,
                                    fill=1.0, base=-96, channel_multiplier=1).then_inc(made, 1)
            nc.gpsimd.affine_select(out=row_low[:], in_=row_low[:], pattern=[[0, 1]], compare_op=ALU.is_ge,
                                    fill=0.0, base=95, channel_multiplier=-1).then_inc(made, 1)
            pool.wait_ge(made, 19)
            nc.gpsimd.affine_select(out=row_low[:], in_=row_low[:], pattern=[[0, 1]], compare_op=ALU.not_equal,
                                    fill=1.0, base=-97, channel_multiplier=1).then_inc(made, 1)
            nc.gpsimd.iota(rank[:], pattern=[[0, G], [-1, E]], base=E, channel_multiplier=0,
                           allow_small_or_imprecise_dtypes=True).then_inc(made, 1)

            def per_tile(stat):
                return stat[:].unsqueeze(2).broadcast_to([P, G, C])

            def tiles(flat):
                return flat.rearrange("p (g c) -> p g c", c=C)

            def center(k, src, b):
                pool.wait_ge(mean_ready[k], b + 1)
                nc.gpsimd.tensor_tensor(tiles(centered[k][:]), tiles(src), per_tile(nmean[k]),
                                        ALU.add).then_inc(center_ready[k], 1)

            def scale(k, dst, b):
                pool.wait_ge(rstd_ready[k], b + 1)
                return nc.gpsimd.tensor_tensor(dst, tiles(centered[k][:]), per_tile(rstd[k]), ALU.mult)

            def iteration(i, front, back):
                g, pos = i - 1, Places(i, front, back)
                if front:
                    pool.wait_ge(narrow_free, pos.n + pos.xt + XT)
                    center(1, x_tok[:, i % 2, :], i)
                    if back:
                        pool.wait_ge(ek_used, KEXP * i)
                    scale(1, xhat[:, :, 0:C], i).then_inc(xhat_ready[1], 1)
                if back:
                    c = Chain(pool, back_p, 3 * g)
                    pool.wait_ge(wide_free, pos.w + pos.norm + NORM)
                    c.inc(nc.gpsimd.tensor_tensor(pairs[:], heads[:, :, 0:2 * C], heads[:, :, 2 * C:4 * C], ALU.add))
                    c.wait()
                    nc.gpsimd.tensor_tensor(tiles(attn[:]), pairs[:, :, 0:C], pairs[:, :, C:2 * C],
                                            ALU.add).then_inc(attn_ready, 1)
                    pool.wait_ge(attn_ready, g + 1)
                    center(2, attn[:], g)
                    c.inc(scale(2, tiles(scaled[:]), g))
                    c.wait()
                    c.inc(nc.gpsimd.tensor_tensor(tiles(gained[:]), tiles(scaled[:]),
                                                  g_rep[:].unsqueeze(1).broadcast_to([P, G, C]), ALU.mult))
                    c.wait()
                    nc.gpsimd.tensor_tensor(x2[:], gained[:], x_tok[:, g % 2, :], ALU.add).then_inc(x2_ready, 1)
                    pool.wait_ge(x2_ready, g + 1)
                    center(3, x2[:], g)
                    scale(3, xhat3[:], g).then_inc(xhat_ready[3], 1)

            run(pool, iteration)

        @block.scalar
        def _(act):
            act.wait_ge(setup_v, SETUP_V)

            def rootinv(k, c, b):
                act.wait_ge(var_ready[k], b + 1)
                c.inc(nc.scalar.activation(lnv[k][:], vari[k][:], ACT.Ln))
                c.wait()
                nc.scalar.activation(r0[k][:], lnv[k][:], ACT.Exp, scale=-0.5).then_inc(r0_ready[k], 1)

            def square(k, b):
                act.wait_ge(center_ready[k], b + 1)
                nc.scalar.activation(squares[k][:], centered[k][:], ACT.Square).then_inc(square_ready[k], 1)

            def copy_stack(k, pos, off):
                for u in range(STACK):
                    act.wait_ge(narrow_full, pos.n + off + u + 1)
                    nc.scalar.copy(stack[k][:, 1024 * u:1024 * u + 1024],
                                   narrow[:, (off + u) % 2, :].bitcast(f16)).then_inc(narrow_free, 1)

            def key_exp(pos, f, units, front_only):
                for u in units:
                    act.wait_ge(narrow_full, pos.n + pos.kexp + u + 1)
                    if not (front_only and u < 2):
                        act.wait_ge(ek_used, KEXP * f + u - 1)
                    nc.scalar.activation(ek[:, u % 2, :, :].rearrange("p a b -> p (a b)"),
                                         narrow[:, (pos.kexp + u) % 2, :], ACT.Exp,
                                         scale=wscale[:, 0:1]).then_inc(narrow_free, 1)

            def iteration(i, front, back):
                f, g, pos = i, i - 1, Places(i, front, back)
                ca = Chain(act, front_a, f)
                cb = Chain(act, back_a, 2 * g)
                if front:
                    for u in range(XT):
                        act.wait_ge(narrow_full, pos.n + pos.xt + u + 1)
                        nc.scalar.copy(x_tok[:, f % 2, 512 * u:512 * u + 512],
                                       narrow[:, (pos.xt + u) % 2, :]).then_inc(narrow_free, 1)
                    square(1, f)
                    rootinv(1, ca, f)
                if back:
                    for u in range(QEXP):
                        act.wait_ge(narrow_full, pos.n + pos.qexp + u + 1)
                        if u >= 2:
                            act.wait_ge(wide_full, pos.w + pos.norm + u - 1)
                        nc.scalar.activation(eq[:, u % 2, :], narrow[:, (pos.qexp + u) % 2, :], ACT.Exp,
                                             scale=wscale[:, 0:1]).then_inc(narrow_free, 1)
                if front:
                    copy_stack(1, pos, pos.stack1)
                    key_exp(pos, f, range(0, 4), not back)
                if back:
                    square(2, g)
                    rootinv(2, cb, g)
                if front:
                    key_exp(pos, f, range(4, KEXP), not back)
                if back:
                    square(3, g)
                    rootinv(3, cb, g)
                    copy_stack(3, pos, pos.stack3)
                    act.wait_ge(gap_ready, g + 1)
                    nc.scalar.activation(e2[:], gap[:], ACT.Exp, scale=wscale[:, 2:3]).then_inc(e2_ready, 1)
                    for u in range(OUTU):
                        act.wait_ge(narrow_full, pos.n + pos.out + u + 1)
                        if u == 0:
                            act.wait_ge(stored, 16 * g)
                        nc.scalar.copy(y_out[:, 512 * u:512 * u + 512],
                                       narrow[:, (pos.out + u) % 2, :]).then_inc(y_ready, 1)
                        act.wait_ge(y_ready, OUTU * g + u + 1)
                        act.sem_inc(narrow_free, 1)

            run(act, iteration)

        @block.vector
        def _(dve):
            st = Chain(dve, setup_v, 0)
            dve.wait_ge(loaded, 16 * 15)
            dve.wait_ge(made, 21)
            for r in range(3):
                st.inc(nc.vector.tensor_copy(qk_nat[:, :, C * r:C * r + C], w_nat[:, 0:2, :]))
            for r in (96, 97):
                st.inc(nc.vector.tensor_copy(qk_nat[:, :, r:r + 1], b_nat[:, 0:2].unsqueeze(2)))
            st.inc(nc.vector.tensor_copy(v_nat[:, 0:C], w_nat[:, 2, :]))
            st.inc(nc.vector.tensor_copy(v_nat[:, C:C + 1], b_nat[:, 2:3]))
            st.inc(nc.vector.tensor_scalar(ctxscale[:], headmask[:], SCALE / N, None, ALU.mult))
            st.inc(nc.vector.scalar_tensor_tensor(ctxbias[:], headmask[:], 1.0 / HEADS,
                                                  bout_rep[:].unsqueeze(1).broadcast_to([P, HEADS, C]),
                                                  ALU.mult, ALU.mult))
            st.inc(nc.vector.tensor_copy(mixz[:, P:P + HEADS], headmask[:, :, 0]))
            dve.wait_ge(setup_t, 1)
            st.inc(nc.vector.tensor_copy(w_rows[:, 0:2 * CH], wide[:, 0, 0:2 * CH]))
            st.inc(nc.vector.tensor_tensor(wo_block[:], headmask[:],
                                           wide[:, 0, 256:256 + C].unsqueeze(1).broadcast_to([P, HEADS, C]),
                                           ALU.mult))
            st.wait()
            for n, (lo, hi) in enumerate(groups):
                st.inc(nc.vector.tensor_reduce(amax[:, n:n + 1], w_rows[:, lo:hi], AX.X, ALU.max,
                                               apply_absolute_value=True))
            dve.wait_ge(setup_t, 2)
            st.inc(nc.vector.tensor_reduce(gmax[:], wide[0:3, 1, 0:P], AX.X, ALU.max))
            st.inc(nc.vector.tensor_copy(u_mat[:], wide[0:C + 1, 1, 512:512 + P]))
            st.wait()
            st.inc(nc.vector.tensor_scalar(gmax[:], gmax[:], 1e-30, None, ALU.max))
            st.wait()
            st.inc(nc.vector.tensor_scalar(gpow[:].bitcast(u32), gmax[:].bitcast(u32), 0x7F800000, None,
                                           ALU.bitwise_and))
            st.wait()
            st.inc(nc.vector.tensor_scalar(gdiag[:], ident[0:3, 0:3], gpow[:], None, ALU.mult))
            dve.wait_ge(setup_t, 3)
            st.inc(nc.vector.tensor_copy(wscale[:], wide[:, 0, 0:3]))
            st.wait()
            st.inc(nc.vector.reciprocal(winv[:], wscale[:]))
            st.wait()
            for n, (lo, hi) in enumerate(groups):
                st.inc(nc.vector.tensor_scalar(w_rows[:, lo:hi], w_rows[:, lo:hi], winv[:, n:n + 1], None, ALU.mult))
            st.wait()
            st.inc(nc.vector.tensor_copy(w_high[:], w_rows[:]))
            st.wait()
            st.inc(nc.vector.tensor_tensor(w_low[:], w_rows[:], w_high[:], ALU.subtract))
            st.wait()
            st.inc(nc.vector.tensor_scalar(w_high[:], w_high[:], row_high[:], None, ALU.mult))
            st.wait()
            st.inc(nc.vector.scalar_tensor_tensor(w_stack[:], w_low[:], row_low[:], w_high[:], ALU.mult, ALU.add))
            st.wait()
            assert st.n == SETUP_V, st.n

            def tiles(flat):
                return flat.rearrange("p (g c) -> p g c", c=C)

            def over_experts(stat):
                return stat[:].unsqueeze(2).broadcast_to([P, G, E])

            def mean(k, c, src):
                c.inc(nc.vector.tensor_reduce(nsum[k][:], tiles(src), AX.X, ALU.add, negate=True))
                c.wait()
                nc.vector.tensor_scalar(nmean[k][:], nsum[k][:], 1.0 / C, None, ALU.mult).then_inc(mean_ready[k], 1)

            def variance(k, c, b, eps):
                dve.wait_ge(square_ready[k], b + 1)
                c.inc(nc.vector.tensor_reduce(vsum[k][:], tiles(squares[k][:]), AX.X, ALU.add))
                c.wait()
                nc.vector.tensor_scalar(vari[k][:], vsum[k][:], 1.0 / C, eps, ALU.mult,
                                        ALU.add).then_inc(var_ready[k], 1)

            def refine(k, c, b):
                dve.wait_ge(r0_ready[k], b + 1)
                c.inc(nc.vector.tensor_tensor(rr[k][:], r0[k][:], r0[k][:], ALU.mult))
                c.wait()
                c.inc(nc.vector.scalar_tensor_tensor(ru[k][:], rr[k][:], -0.5, vari[k][:], ALU.mult, ALU.mult))
                c.wait()
                nc.vector.scalar_tensor_tensor(rstd[k][:], ru[k][:], 1.5, r0[k][:], ALU.add,
                                               ALU.mult).then_inc(rstd_ready[k], 1)

            def split(k, c, b, src):
                dve.wait_ge(xhat_ready[k], b + 1)
                c.inc(nc.vector.tensor_copy(parts[k][:, :, 0:C], src))
                nc.vector.tensor_copy(parts[k][:, :, 2 * C:3 * C], src).then_inc(parts_ready[k], 1)
                c.wait()
                nc.vector.tensor_tensor(parts[k][:, :, C:2 * C], src, parts[k][:, :, 0:C],
                                        ALU.subtract).then_inc(parts_ready[k], 1)

            def query_max(pos, c, g):
                for u in range(QMAX):
                    dve.wait_ge(wide_full, pos.w + pos.qmax + u + 1)
                    half = u // 2
                    nc.vector.tensor_reduce(nqmax[:, half, 32 * (u % 2):32 * (u % 2) + 32],
                                            wide[:, (pos.qmax + u) % 2, :].rearrange("p (a d) -> p a d", d=DH),
                                            AX.X, ALU.max, negate=True).then_inc(wide_free, 1)
                    if u % 2:
                        dve.wait_ge(wide_free, pos.w + pos.qmax + u + 1)
                        c.inc(nc.vector.tensor_copy(qmax_nat[:, half, 0, :], nqmax[:, half, :]))
                        c.wait()
                        nc.vector.tensor_tensor(qmax_nat[:, half, 1, :], nqmax[:, half, :], qmax_nat[:, half, 0, :],
                                                ALU.subtract).then_inc(qmax_nat_ready, 1)
                for half in range(2):
                    dve.wait_ge(small_full, pos.s + pos.qtr + half + 1)
                    nc.vector.tensor_copy(qmax_tr[:, half, :],
                                          small[:, 0:P // 2].bitcast(f16)).then_inc(small_free, 1)

            def normalise(pos, c, units):
                for u in units:
                    dve.wait_ge(wide_full, pos.w + pos.norm + u + 1)
                    src = wide[:, (pos.norm + u) % 2, :].rearrange("p (t c) -> p t c", t=4)
                    c.inc(nc.vector.reciprocal(zrec[:, u % 2, :, :], src[:, :, P:P + HEADS]))
                    c.wait()
                    nc.vector.tensor_tensor(
                        heads[:, 4 * u:4 * u + 4, :].rearrange("p t (h c) -> p t h c", h=HEADS),
                        src[:, :, 0:P].rearrange("p t (h c) -> p t h c", h=HEADS),
                        zrec[:, u % 2, :, :].unsqueeze(3).broadcast_to([P, 4, HEADS, C]),
                        ALU.mult).then_inc(wide_free, 1)

            def key_max(pos, c):
                for u in range(KMAX):
                    dve.wait_ge(wide_full, pos.w + pos.kmax + u + 1)
                    nc.vector.tensor_reduce(kmax[:, u:u + 1], wide[:, (pos.kmax + u) % 2, :], AX.X,
                                            ALU.max).then_inc(wide_free, 1)
                dve.wait_ge(wide_free, pos.w + pos.kmax + KMAX)
                c.inc(nc.vector.tensor_reduce(nkmax[:], kmax[:], AX.X, ALU.max, negate=True))
                c.wait()
                c.inc(nc.vector.tensor_copy(kmax_nat[:, 98:99], nkmax[:]))
                c.wait()
                nc.vector.tensor_tensor(kmax_nat[:, 99:100], nkmax[:], kmax_nat[:, 98:99],
                                        ALU.subtract).then_inc(kmax_nat_ready, 1)
                dve.wait_ge(small_full, pos.s + pos.ktr + 1)
                nc.vector.tensor_tensor(ws_kmax[:], ws_k, small[:, 0:P // 2].bitcast(f16),
                                        ALU.add).then_inc(small_free, 1)

            def context(pos, c, f):
                dve.wait_ge(ek_used, KEXP * f + KEXP)
                c.inc(nc.vector.reciprocal(grec[:], ctxsum[:, C:C + 1]))
                c.wait()
                nc.vector.tensor_scalar(gnat[:, 0:C + 1], ctxsum[:, 0:C + 1], grec[:], None, ALU.mult).then_inc(ctx_free, 1)
                dve.wait_ge(small_full, pos.s + pos.gtr + 1)
                nc.vector.tensor_copy(gtr[:], small[0:C + 1, 0:P]).then_inc(small_free, 1)
                dve.wait_ge(small_full, pos.s + pos.mix + 1)
                nc.vector.tensor_tensor(mix[:], small[:, 0:P], ctxscale[:].rearrange("p h c -> p (h c)"),
                                        ALU.mult).then_inc(small_free, 1)
                dve.wait_ge(small_free, pos.s + pos.mix + 1)
                nc.vector.tensor_tensor(mixz[:, 0:P], mix[:], ctxbias[:].rearrange("p h c -> p (h c)"),
                                        ALU.add).then_inc(mixz_ready, 1)

            def route(pos, c, g):
                dve.wait_ge(small_full, pos.s + pos.logit + 1)
                nc.vector.tensor_copy(logit[:].rearrange("p g e -> p (g e)"), small[:, 0:G * E]).then_inc(small_free, 1)
                dve.wait_ge(small_free, pos.s + pos.logit + 1)

                def step(ins):
                    c.inc(ins)
                    c.wait()

                step(nc.vector.tensor_reduce(top1[:], logit[:], AX.X, ALU.max))
                step(nc.vector.tensor_tensor(tie1[:], logit[:], over_experts(top1), ALU.is_equal))
                step(nc.vector.tensor_tensor(tie1[:], tie1[:], rank[:], ALU.mult))
                step(nc.vector.tensor_reduce(pick1[:], tie1[:], AX.X, ALU.max))
                step(nc.vector.tensor_tensor(one1[:], tie1[:], over_experts(pick1), ALU.is_equal))
                step(nc.vector.scalar_tensor_tensor(logit2[:].rearrange("p g e -> p (g e)"),
                                                    one1[:].rearrange("p g e -> p (g e)"), -3.0e38,
                                                    logit[:].rearrange("p g e -> p (g e)"), ALU.mult, ALU.add))
                step(nc.vector.tensor_reduce(top2[:], logit2[:], AX.X, ALU.max))
                nc.vector.tensor_tensor(gap[:], top2[:], top1[:], ALU.subtract).then_inc(gap_ready, 1)
                step(nc.vector.tensor_tensor(tie2[:], logit2[:], over_experts(top2), ALU.is_equal))
                step(nc.vector.tensor_tensor(tie2[:], tie2[:], rank[:], ALU.mult))
                step(nc.vector.tensor_reduce(pick2[:], tie2[:], AX.X, ALU.max))
                step(nc.vector.tensor_tensor(one2[:], tie2[:], over_experts(pick2), ALU.is_equal))
                dve.wait_ge(e2_ready, g + 1)
                step(nc.vector.tensor_scalar(den[:], e2[:], 1.0, None, ALU.add))
                step(nc.vector.reciprocal(g1[:], den[:]))
                step(nc.vector.tensor_scalar(g1[:], g1[:], wscale[:, 1:2], None, ALU.mult))
                step(nc.vector.tensor_tensor(g2[:], g1[:], e2[:], ALU.mult))
                step(nc.vector.tensor_tensor(one1[:], one1[:], over_experts(g1), ALU.mult))
                step(nc.vector.tensor_tensor(one2[:], one2[:], over_experts(g2), ALU.mult))
                step(nc.vector.tensor_tensor(gates[:], one1[:], one2[:], ALU.add))

            def gate(pos, g):
                for u in range(GATE):
                    dve.wait_ge(wide_full, pos.w + pos.gate + u + 1)
                    dve.wait_ge(gated_used, max(0, u - 1) + GATE * g)
                    nc.vector.tensor_tensor(
                        gated[:, u % 2, :, :, :].rearrange("p e t c -> p t e c"), wide[:, (pos.gate + u) % 2, :].rearrange(
                            "p (t e c) -> p t e c", t=4, e=E),
                        gates[:, 4 * u:4 * u + 4, :].unsqueeze(3).broadcast_to([P, 4, E, C]),
                        ALU.mult).then_inc(wide_free, 1)

            def iteration(i, front, back):
                f, g, pos = i, i - 1, Places(i, front, back)
                cf, cb = Chain(dve, front_v, FRONT_V * f), Chain(dve, back_v, BACK_V * g)
                if front:
                    dve.wait_ge(narrow_free, pos.n + pos.xt + XT)
                    mean(1, cf, x_tok[:, f % 2, :])
                if back:
                    query_max(pos, cb, g)
                if front:
                    variance(1, cf, f, EPS_IN)
                    refine(1, cf, f)
                if back:
                    normalise(pos, cb, range(0, 4))
                if front:
                    split(1, cf, f, xhat[:, :, 0:C])
                if back:
                    normalise(pos, cb, range(4, NORM))
                if front:
                    key_max(pos, cf)
                if back:
                    dve.wait_ge(attn_ready, g + 1)
                    mean(2, cb, attn[:])
                    variance(2, cb, g, EPS)
                    refine(2, cb, g)
                if front:
                    context(pos, cf, f)
                    assert cf.n == FRONT_V, cf.n
                if back:
                    dve.wait_ge(x2_ready, g + 1)
                    mean(3, cb, x2[:])
                    variance(3, cb, g, EPS)
                    refine(3, cb, g)
                    split(3, cb, g, xhat3[:])
                    route(pos, cb, g)
                    gate(pos, g)
                    assert cb.n == BACK_V, cb.n

            run(dve, iteration)

        @block.tensor
        def _(pe):
            def mm(dst, lhs, rhs, start=True, stop=True):
                return nc.tensor.matmul(dst, lhs, rhs, start=start, stop=stop)

            def tr(dst, src, idt, start=True, stop=True):
                return nc.tensor.matmul(dst, src, idt, is_transpose=True, start=start, stop=stop)

            pe.wait_ge(made, 11)
            pe.wait_ge(setup_v, 7)
            for s in range(2):
                tr(wide[:, 0, P * s:P * s + P], qk_nat[:, s, :], ident[:])
            tr(wide[:, 0, 256:256 + C], wo_nat[:, :], ident[0:C, 0:C]).then_inc(setup_t, 1)
            pe.wait_ge(setup_v, 15)
            tr(wide[0:3, 1, 0:P], amax[:, :], ident[:])
            mm(wide[0:C + 1, 1, 512:512 + P], v_nat[:, :],
               wo_block[:].rearrange("p h c -> p (h c)")).then_inc(setup_t, 1)
            pe.wait_ge(setup_v, 20)
            mm(wide[:, 0, 0:3], ones[0:3, :], gdiag[:, :]).then_inc(setup_t, 1)
            pe.wait_ge(setup_v, SETUP_V)

            def to_tokens(pos, f):
                pe.wait_ge(x_loaded, 16 * f + 16)
                for u in range(XT):
                    wait_slot(pe, narrow_free, pos.n + pos.xt + u, 2)
                    for t in range(4):
                        ins = tr(narrow[:, (pos.xt + u) % 2, P * t:P * t + P],
                                 x_in[:, 512 * u + P * t:512 * u + P * t + P], ident[:])
                    ins.then_inc(narrow_full, 1)

            def query_logits_by_token(pos):
                for u in range(QMAX):
                    wait_slot(pe, wide_free, pos.w + pos.qmax + u, 2)
                    for t in range(8):
                        tile = P * (8 * u + t)
                        ins = mm(wide[:, (pos.qmax + u) % 2, P * t:P * t + P], stack[1][:, tile:tile + P], ws_q)
                    ins.then_inc(wide_full, 1)

            def query_max_rows(pos, g):
                for half in range(2):
                    pe.wait_ge(qmax_nat_ready, 2 * g + half + 1)
                    wait_slot(pe, small_free, pos.s + pos.qtr + half, 1)
                    tr(small[:, 0:P // 2].bitcast(f16),
                       qmax_nat[:, half, :, :].rearrange("p a b -> p (a b)"), ident16[:]).then_inc(small_full, 1)

            def attend(pos, u):
                pe.wait_ge(narrow_free, pos.n + pos.qexp + u + 1)
                wait_slot(pe, wide_free, pos.w + pos.norm + u, 2)
                for t in range(4):
                    ins = mm(wide[:, (pos.norm + u) % 2, 256 * t:256 * t + P + HEADS],
                             eq[:, u % 2, P * t:P * t + P], mixz[:, :])
                ins.then_inc(wide_full, 1)

            def query_side(pos, g):
                pe.wait_ge(mixz_ready, g + 1)
                for u in range(QEXP):
                    half = u // 4
                    wait_slot(pe, narrow_free, pos.n + pos.qexp + u, 2)
                    pe.wait_ge(small_free, pos.s + pos.qtr + half + 1)
                    slot = (pos.qexp + u) % 2
                    mm(narrow[:, slot, :], ws_q, stack[1][:, 512 * u:512 * u + 512], stop=False)
                    for t in range(4):
                        ins = mm(narrow[:, slot, P * t:P * t + P], maxpick[:, 4 * (u % 4) + t, :],
                                 qmax_tr[:, half, :], start=False, stop=(t == 3))
                    ins.then_inc(narrow_full, 1)
                    if u:
                        attend(pos, u - 1)
                attend(pos, QEXP - 1)

            def make_stack(k, pos, off, b):
                pe.wait_ge(parts_ready[k], 2 * b + 2)
                for u in range(STACK):
                    wait_slot(pe, narrow_free, pos.n + off + u, 2)
                    for t in range(8):
                        ins = tr(narrow[:, (off + u) % 2, P // 2 * t:P // 2 * t + P // 2].bitcast(f16),
                                 parts[k][:, 8 * u + t, :], ident16[:])
                    ins.then_inc(narrow_full, 1)

            def key_logits_by_channel(pos):
                for u in range(KMAX):
                    pe.wait_ge(narrow_free, pos.n + pos.stack1 + u + 1)
                    wait_slot(pe, wide_free, pos.w + pos.kmax + u, 2)
                    for h in range(2):
                        at = 1024 * u + 512 * h
                        ins = mm(wide[:, (pos.kmax + u) % 2, 512 * h:512 * h + 512], ws_k, stack[1][:, at:at + 512])
                    ins.then_inc(wide_full, 1)

            def sum_context(pos, u):
                pe.wait_ge(narrow_free, pos.n + pos.kexp + u + 1)
                for t in range(4):
                    ins = mm(ctxsum[:, 0:C + 1], ek[:, u % 2, t, :], xhat[:, 4 * u + t, :],
                             start=(u == 0 and t == 0), stop=(u == KEXP - 1 and t == 3))
                ins.then_inc(ek_used, 1)

            def key_side(pos, f, front_only):
                pe.wait_ge(kmax_nat_ready, f + 1)
                wait_slot(pe, small_free, pos.s + pos.ktr, 1)
                tr(small[:, 0:P // 2].bitcast(f16), kmax_nat[:, :], ident16[:]).then_inc(small_full, 1)
                pe.wait_ge(small_free, pos.s + pos.ktr + 1)
                if not front_only:
                    pe.wait_ge(ctx_free, f)
                for u in range(KEXP):
                    wait_slot(pe, narrow_free, pos.n + pos.kexp + u, 2)
                    for t in range(4):
                        tile = P * (4 * u + t)
                        ins = mm(narrow[:, (pos.kexp + u) % 2, P * t:P * t + P], stack[1][:, tile:tile + P], ws_kmax[:])
                    ins.then_inc(narrow_full, 1)
                    if u:
                        sum_context(pos, u - 1)
                sum_context(pos, KEXP - 1)
                pe.wait_ge(ctx_free, f + 1)
                wait_slot(pe, small_free, pos.s + pos.gtr, 1)
                tr(small[:, 0:P], gnat[:, :], ident[:]).then_inc(small_full, 1)
                pe.wait_ge(small_free, pos.s + pos.gtr + 1)
                mm(small[:, 0:P], gtr[:, :], u_mat[:, :]).then_inc(small_full, 1)

            def experts(pos, g):
                pe.wait_ge(narrow_free, pos.n + pos.stack3 + STACK)
                wait_slot(pe, small_free, pos.s + pos.logit, 1)
                for t in range(G):
                    ins = mm(small[:, E * t:E * t + E], stack[3][:, P * t:P * t + P], ws_r)
                ins.then_inc(small_full, 1)
                for u in range(GATE + 1):
                    if u < GATE:
                        wait_slot(pe, wide_free, pos.w + pos.gate + u, 2)
                        for t in range(4):
                            tile = P * (4 * u + t)
                            ins = mm(wide[:, (pos.gate + u) % 2, 256 * t:256 * t + 256],
                                     stack[3][:, tile:tile + P], ws_e)
                        ins.then_inc(wide_full, 1)
                    if u:
                        add_experts(pos, g, u - 1)

            def add_experts(pos, g, v):
                pe.wait_ge(wide_free, pos.w + pos.gate + v + 1)
                if v % 4 == 0:
                    wait_slot(pe, narrow_free, pos.n + pos.out + v // 4, 2)
                dst = narrow[:, (pos.out + v // 4) % 2, P * (v % 4):P * (v % 4) + P]
                for e in range(E):
                    ins = tr(dst, gated[:, v % 2, e, :, :].rearrange("p t c -> p (t c)"), ident[:], start=(e == 0), stop=False)
                ins.then_inc(gated_used, 1)
                ins = tr(dst, x2[:, P * v:P * v + P], ident[:], start=False, stop=True)
                if v % 4 == 3:
                    ins.then_inc(narrow_full, 1)

            def iteration(i, front, back):
                f, g, pos = i, i - 1, Places(i, front, back)
                if front:
                    to_tokens(pos, f)
                if back:
                    query_logits_by_token(pos)
                    query_max_rows(pos, g)
                    query_side(pos, g)
                if front:
                    make_stack(1, pos, pos.stack1, f)
                    key_logits_by_channel(pos)
                    key_side(pos, f, not back)
                if back:
                    make_stack(3, pos, pos.stack3, g)
                    experts(pos, g)

            run(pe, iteration)


_INS = ['x', 'L0_conv_w_qkv', 'L0_conv_b_qkv', 'L0_conv_w_out', 'L0_conv_b_out', 'L0_conv_g_ln',
        'L0_ffn_router_w', 'L0_ffn_router_b', 'L0_ffn_expert_w', 'L0_ffn_expert_b']


def kernel(**inputs):
    import numpy as _np
    import concourse.bacc as _bacc
    from concourse import mybir as _mybir
    from concourse.bass_utils import run_bass_kernel_spmd as _run
    nc = _bacc.Bacc("TRN2", target_bir_lowering=False, num_devices=1)
    arrays, args = {}, []
    for name in _INS:
        a = _np.ascontiguousarray(inputs[name])
        arrays[f"in_{name}_dram"] = a
        args.append(nc.dram_tensor(f"in_{name}_dram", a.shape, _mybir.dt.from_np(a.dtype), kind="ExternalInput").ap())
    out = nc.dram_tensor("out_dram", (8, 32, 64, 64), _mybir.dt.float32, kind="ExternalOutput").ap()
    build(nc, *args, out)
    r = _run(nc, [arrays], core_ids=[0])
    return r.results[0]["out_dram"]
```

```python
import concourse.bass as bass
from concourse import mybir
from contextlib import ExitStack

NB, C, N = 8, 32, 4096
HEADS, DH = 4, 32
CH = HEADS * DH
P = 128
G = N // P
J = P // C
T = G // J
E = 8
EPS = 1e-5
EPS_IN = 1e-6
SCALE = DH ** -0.5

QMAX, NORM, KMAX, GATE = 4, 8, 4, 8
QEXP, XT, STACK, KEXP, OUTU = 8, 2, 4, 8, 2
STEPS = range(QEXP + 4)
LAG = 4
AT_STACK3, AT_ROUTE = 2, 3
SETUP_V = 34


def build(nc, x, w_qkv, b_qkv, w_out, b_out, g_ln, router_w, router_b, expert_w, expert_b, out):
    f32, f16, u32, i32 = mybir.dt.float32, mybir.dt.float16, mybir.dt.uint32, mybir.dt.int32
    ALU, ACT, AX = mybir.AluOpType, mybir.ActivationFunctionType, mybir.AxisListType
    x_v = x.rearrange("b c (j t) f -> b j c (t f)", j=J)
    out_v = out.rearrange("b c (j t) f -> b j c (t f)", j=J)

    ctx = ExitStack()
    with ctx:
        def sb(name, shape, dt=f32):
            return ctx.enter_context(nc.sbuf_tensor(name, shape, dt))

        def sem(name):
            return ctx.enter_context(nc.semaphore(name))

        ident = sb("ident", [P, P])
        ident16 = sb("ident16", [P, P], f16)
        ones = sb("ones", [P, P])
        headmask = sb("headmask", [P, HEADS, C])
        ctxscale = sb("ctxscale", [P, HEADS, C])
        ctxbias = sb("ctxbias", [P, HEADS, C])
        bout_rep = sb("bout_rep", [P, C])
        bout_mean = sb("bout_mean", [P, 1])
        bout_centered = sb("bout_centered", [P, C])
        g_rep = sb("g_rep", [P, C])
        u_mean = sb("u_mean", [C + 1, HEADS])
        maxpick = sb("maxpick", [P, 16, CH], f16)
        rank = sb("rank", [P, G, E])
        row_high = sb("row_high", [P, 1])
        row_low = sb("row_low", [P, 1])
        w_nat = sb("w_nat", [P, 3, C])
        b_nat = sb("b_nat", [P, 3])
        qk_nat = sb("qk_nat", [P, 2, P])
        v_nat = sb("v_nat", [P, C + 1])
        wo_nat = sb("wo_nat", [C, P])
        wo_block = sb("wo_block", [P, HEADS, C])
        u_mat = sb("u_mat", [C + 1, P])
        NW = 2 * CH + E * C + E
        w_rows = sb("w_rows", [P, NW])
        w_high = sb("w_high", [P, NW], f16)
        w_low = sb("w_low", [P, NW], f16)
        w_stack = sb("w_stack", [P, NW], f16)
        groups = [(0, 2 * CH), (2 * CH, 2 * CH + E * C), (2 * CH + E * C, NW)]
        amax = sb("amax", [P, 3])
        gmax = sb("gmax", [3, 1])
        gpow = sb("gpow", [3, 1])
        gdiag = sb("gdiag", [3, 3])
        wscale = sb("wscale", [P, 3])
        winv = sb("winv", [P, 3])
        ws_q = w_stack[:, 0:CH]
        ws_k = w_stack[:, CH:2 * CH]
        ws_e = w_stack[:, 2 * CH:2 * CH + E * C]
        ws_r = w_stack[:, 2 * CH + E * C:NW]
        x_in = sb("x_in", [P, N // J])
        x_tok = sb("x_tok", [P, 2, G * C])
        LN = (1, 2, 3)
        centered = {k: sb(f"centered{k}", [P, G * C]) for k in LN}
        squares = {k: sb(f"squares{k}", [P, G * C]) for k in LN}
        nsum = {k: sb(f"nsum{k}", [P, G]) for k in LN}
        nmean = {k: sb(f"nmean{k}", [P, G]) for k in LN}
        vsum = {k: sb(f"vsum{k}", [P, G]) for k in LN}
        vari = {k: sb(f"vari{k}", [P, G]) for k in LN}
        root = {k: sb(f"root{k}", [P, G]) for k in LN}
        rr = {k: sb(f"rr{k}", [P, G]) for k in LN}
        ru = {k: sb(f"ru{k}", [P, G]) for k in LN}
        rstd = {k: sb(f"rstd{k}", [P, G]) for k in LN}
        xhat = sb("xhat", [P, G, C + 1])
        xhat3 = sb("xhat3", [P, G, C])
        parts = {k: sb(f"parts{k}", [P, G, P], f16) for k in (1, 3)}
        stack = {k: sb(f"stack{k}", [P, N], f16) for k in (1, 3)}
        kmax = sb("kmax", [P, KMAX])
        nkmax = sb("nkmax", [P, 1])
        kmax_nat = sb("kmax_nat", [P, P], f16)
        ws_kmax = sb("ws_kmax", [P, CH], f16)
        ek = sb("ek", [P, 2, 4, CH])
        gnat = sb("gnat", [P, P])
        grec = sb("grec", [P, 1])
        gtr = sb("gtr", [C + 1, P])
        mix = sb("mix", [P, P])
        mixz = sb("mixz", [P, P + HEADS])
        nqmax = sb("nqmax", [P, 2, 16 * HEADS])
        qmax_nat = sb("qmax_nat", [P, 2, 2, 16 * HEADS], f16)
        qmax_tr = sb("qmax_tr", [P, 2, P], f16)
        eq = sb("eq", [P, 2, 4 * P])
        zrec = sb("zrec", [P, 2, 4, HEADS])
        heads = sb("heads", [P, G, CH])
        pairs = sb("pairs", [P, G, 2 * C])
        scaled = sb("scaled", [P, G * C])
        gained = sb("gained", [P, G * C])
        x2 = sb("x2", [P, G * C])
        logit = sb("logit", [P, G, E])
        logit2 = sb("logit2", [P, G, E])
        tie1 = sb("tie1", [P, G, E])
        tie2 = sb("tie2", [P, G, E])
        one1 = sb("one1", [P, G, E])
        one2 = sb("one2", [P, G, E])
        gates = sb("gates", [P, G, E])
        top1 = sb("top1", [P, G])
        top2 = sb("top2", [P, G])
        pick1 = sb("pick1", [P, G])
        pick2 = sb("pick2", [P, G])
        gap = sb("gap", [P, G])
        e2 = sb("e2", [P, G])
        den = sb("den", [P, G])
        g1 = sb("g1", [P, G])
        g2 = sb("g2", [P, G])
        gated = sb("gated", [P, 2, E, 4, C])
        y_out = sb("y_out", [P, N // J])

        wide = ctx.enter_context(nc.psum_tensor("wide", [P, 2, 1024], f32))
        narrow = ctx.enter_context(nc.psum_tensor("narrow", [P, 2, 512], f32))
        sums = ctx.enter_context(nc.psum_tensor("sums", [P, 512], f32))
        small = ctx.enter_context(nc.psum_tensor("small", [P, 512], f32))

        loaded = sem("weights_loaded")
        made = sem("constants_made")
        setup_v = sem("setup_vector_steps")
        setup_t = sem("setup_tensor_steps")
        x_loaded = sem("x_loaded")
        stored = sem("stored")
        wide_full, wide_free = sem("wide_full"), sem("wide_free")
        narrow_full, narrow_free = sem("narrow_full"), sem("narrow_free")
        small_full, small_free = sem("small_full"), sem("small_free")
        ctx_free = sem("ctx_free")
        mean_ready = {k: sem(f"mean_ready{k}") for k in (1, 3)}
        center_ready = {k: sem(f"center_ready{k}") for k in LN}
        square_ready = {k: sem(f"square_ready{k}") for k in LN}
        rstd_ready = {k: sem(f"rstd_ready{k}") for k in LN}
        xhat_ready = {k: sem(f"xhat_ready{k}") for k in LN}
        parts_ready = {k: sem(f"parts_ready{k}") for k in (1, 3)}
        kmax_nat_ready = sem("kmax_nat_ready")
        ek_used = sem("ek_used")
        mixz_ready = sem("mixz_ready")
        qmax_nat_ready = sem("qmax_nat_ready")
        x2_ready = sem("x2_ready")
        gap_ready, e2_ready = sem("gap_ready"), sem("e2_ready")
        gated_used = sem("gated_used")
        out_full = sem("out_full")
        y_ready = sem("y_ready")
        y_free = sem("y_free")
        ln1_v, kq_v = sem("layernorm1_vector_steps"), sem("key_query_vector_steps")
        ln23_v, route_v = sem("layernorm23_vector_steps"), sem("route_vector_steps")
        heads_p, ln2_p = sem("heads_pool_steps"), sem("layernorm2_pool_steps")
        LN1_V, KQ_V, LN23_V, ROUTE_V = 13, 13, 24, 18

        class Chain:

            def __init__(self, eng, s, base):
                self.eng, self.s, self.base, self.n = eng, s, base, 0

            def inc(self, ins):
                ins.then_inc(self.s, 1)
                self.n += 1
                return self

            def wait(self):
                self.eng.wait_ge(self.s, self.base + self.n)

        class Places:

            def __init__(self, i, cur, prev, nxt):
                if isinstance(i, int):
                    a, b, c = max(min(i + 1, NB), 0), max(min(i, NB), 0), max(i - 1, 0)
                    self.w, self.n, self.s = 16 * b + 8 * c, 2 * a + 20 * b + 4 * c, 5 * b + c
                else:
                    self.w, self.n, self.s = 24 * i - 8, 26 * i - 2, 6 * i - 1
                w = n = s = 0
                if cur:
                    self.stack1, n = n, n + STACK
                    self.kmax, w = w, w + KMAX
                    self.qmax, w = w, w + QMAX
                    self.ktr, self.qtr, self.gtr, self.mix, s = 0, 1, 3, 4, 5
                    self.kexp, n = n, n + KEXP
                if nxt:
                    self.xt, n = n, n + XT
                self.logit = s
                self.qexp, self.norm, self.gate = {}, {}, {}
                for step in STEPS:
                    if prev and step == AT_STACK3:
                        self.stack3, n = n, n + STACK
                    if cur and step < QEXP:
                        self.qexp[step], n = n, n + 1
                    if cur and 0 <= step - 1 < NORM:
                        self.norm[step - 1], w = w, w + 1
                    if prev and 0 <= step - LAG < GATE:
                        self.gate[step - LAG], w = w, w + 1

        def run(engine, iteration):
            iteration(-1, False, False, True)
            iteration(0, True, False, True)
            with engine.Fori(1, NB - 1) as i:
                iteration(i, True, True, True)
            iteration(NB - 1, True, True, False)
            iteration(NB, False, True, False)

        def wait_slot(eng, free, at, slots):
            if isinstance(at, int) and at < slots:
                return
            eng.wait_ge(free, at - slots + 1)

        block = ctx.enter_context(nc.Block())

        @block.sync
        def _(sp):
            def load(b):
                sp.dma_start(x_in[:, :], x_v[bass.ds(b, 1)].rearrange("b j c i -> (b j) c i")).then_inc(x_loaded, 16)

            load(0)
            sp.dma_start(w_nat[:, :, :], w_qkv.rearrange("(s p) c -> p s c", p=P)).then_inc(loaded, 16)
            sp.dma_start(b_nat[:, :], b_qkv.rearrange("(s p) -> p s", p=P),
                         allow_slow_non_contiguous=True).then_inc(loaded, 16)
            sp.dma_start(wo_nat[:, :], w_out).then_inc(loaded, 16)
            sp.dma_start(bout_rep[:, :], b_out.partition_broadcast(P)).then_inc(loaded, 16)
            sp.dma_start(g_rep[:, :], g_ln.partition_broadcast(P)).then_inc(loaded, 16)
            sp.wait_ge(made, 1)
            lo, hi = groups[1]
            for r in range(3):
                rows = slice(C * r, C * r + C)
                sp.dma_start(w_rows[rows, lo:hi].rearrange("d (e c) -> d e c", e=E),
                             expert_w.rearrange("e d c -> d e c")).then_inc(loaded, 16)
                sp.dma_start(w_rows[rows, hi:NW], router_w).then_inc(loaded, 16)
            for r in (96, 97):
                sp.dma_start(w_rows[r:r + 1, lo:hi],
                             expert_b.rearrange("e c -> (e c)").unsqueeze(0)).then_inc(loaded, 16)
                sp.dma_start(w_rows[r:r + 1, hi:NW], router_b.unsqueeze(0)).then_inc(loaded, 16)

            def store(b):
                sp.wait_ge(y_ready, OUTU * b + OUTU)
                sp.dma_start(out_v[bass.ds(b, 1)].rearrange("b j c i -> (b j) c i"), y_out[:, :]).then_inc(stored, 16)
                sp.wait_ge(stored, 16 * b + 16)
                sp.sem_inc(y_free, 1)

            def load_next(b):
                sp.wait_ge(mean_ready[1], b)
                load(b)

            sp.sem_inc(y_free, 1)
            load_next(1)
            load_next(2)
            with sp.Fori(1, NB - 2) as i:
                load_next(i + 2)
                store(i - 1)
            for b in range(NB - 3, NB):
                store(b)

        @block.gpsimd
        def _(pool):
            nc.gpsimd.memset(w_rows[:], 0.0).then_inc(made, 1)
            nc.gpsimd.memset(ones[:], 1.0).then_inc(made, 1)
            nc.gpsimd.memset(maxpick[:], 0.0).then_inc(made, 1)
            nc.gpsimd.memset(qk_nat[:], 0.0).then_inc(made, 1)
            nc.gpsimd.memset(kmax_nat[:], 0.0).then_inc(made, 1)
            nc.gpsimd.memset(gnat[:], 0.0).then_inc(made, 1)
            nc.gpsimd.memset(xhat[:, :, C:C + 1], 1.0).then_inc(made, 1)
            for k in (1, 3):
                nc.gpsimd.memset(parts[k][:, :, 96:P], 1.0).then_inc(made, 1)
            pool.wait_ge(made, 9)
            nc.gpsimd.affine_select(out=ident[:], in_=ones[:], pattern=[[-1, P]], compare_op=ALU.is_equal,
                                    fill=0.0, base=0, channel_multiplier=1).then_inc(made, 1)
            nc.gpsimd.affine_select(out=ident16[:], in_=ones[:], pattern=[[-1, P]], compare_op=ALU.is_equal,
                                    fill=0.0, base=0, channel_multiplier=1).then_inc(made, 1)
            nc.gpsimd.affine_select(out=headmask[:], in_=ones[:].rearrange("p (h c) -> p h c", h=HEADS),
                                    pattern=[[-DH, HEADS], [0, C]], compare_op=ALU.is_ge,
                                    fill=0.0, base=0, channel_multiplier=1).then_inc(made, 1)
            nc.gpsimd.affine_select(out=maxpick[:].rearrange("p t (h d) -> p t h d", h=HEADS),
                                    in_=maxpick[:].rearrange("p t (h d) -> p t h d", h=HEADS),
                                    pattern=[[-HEADS, 16], [-1, HEADS], [0, DH]], compare_op=ALU.not_equal,
                                    fill=1.0, base=0, channel_multiplier=1).then_inc(made, 1)
            nc.gpsimd.affine_select(out=row_high[:], in_=ones[:, 0:1], pattern=[[0, 1]], compare_op=ALU.is_ge,
                                    fill=0.0, base=63, channel_multiplier=-1).then_inc(made, 1)
            nc.gpsimd.affine_select(out=row_low[:], in_=ones[:, 0:1], pattern=[[0, 1]], compare_op=ALU.is_ge,
                                    fill=0.0, base=-64, channel_multiplier=1).then_inc(made, 1)
            pool.wait_ge(made, 15)
            nc.gpsimd.affine_select(out=headmask[:], in_=headmask[:], pattern=[[DH, HEADS], [0, C]],
                                    compare_op=ALU.is_ge, fill=0.0, base=DH - 1,
                                    channel_multiplier=-1).then_inc(made, 1)
            nc.gpsimd.affine_select(out=maxpick[:].rearrange("p t (h d) -> p t h d", h=HEADS),
                                    in_=maxpick[:].rearrange("p t (h d) -> p t h d", h=HEADS),
                                    pattern=[[-HEADS, 16], [-1, HEADS], [0, DH]], compare_op=ALU.not_equal,
                                    fill=1.0, base=-64, channel_multiplier=1).then_inc(made, 1)
            nc.gpsimd.affine_select(out=row_high[:], in_=row_high[:], pattern=[[0, 1]], compare_op=ALU.not_equal,
                                    fill=1.0, base=-96, channel_multiplier=1).then_inc(made, 1)
            nc.gpsimd.affine_select(out=row_low[:], in_=row_low[:], pattern=[[0, 1]], compare_op=ALU.is_ge,
                                    fill=0.0, base=95, channel_multiplier=-1).then_inc(made, 1)
            pool.wait_ge(made, 19)
            nc.gpsimd.affine_select(out=row_low[:], in_=row_low[:], pattern=[[0, 1]], compare_op=ALU.not_equal,
                                    fill=1.0, base=-97, channel_multiplier=1).then_inc(made, 1)
            nc.gpsimd.iota(rank[:], pattern=[[0, G], [-1, E]], base=E, channel_multiplier=0,
                           allow_small_or_imprecise_dtypes=True).then_inc(made, 1)

            def per_tile(stat):
                return stat[:].unsqueeze(2).broadcast_to([P, G, C])

            def tiles(flat):
                return flat.rearrange("p (g c) -> p g c", c=C)

            def center(k, src, b):
                pool.wait_ge(mean_ready[k], b + 1)
                nc.gpsimd.tensor_tensor(tiles(centered[k][:]), tiles(src), per_tile(nmean[k]),
                                        ALU.add).then_inc(center_ready[k], 1)

            def scale(k, dst, b):
                pool.wait_ge(rstd_ready[k], b + 1)
                return nc.gpsimd.tensor_tensor(dst, tiles(centered[k][:]), per_tile(rstd[k]), ALU.mult)

            def sum_heads(pos, c, f, q):
                pool.wait_ge(wide_free, pos.w + pos.norm[2 * q + 1] + 1)
                here = slice(8 * q, 8 * q + 8)
                c.inc(nc.gpsimd.tensor_tensor(pairs[:, here, :], heads[:, here, 0:2 * C], heads[:, here, 2 * C:4 * C],
                                              ALU.add))
                c.wait()
                c.inc(nc.gpsimd.tensor_tensor(tiles(centered[2][:])[:, here, :], pairs[:, here, 0:C],
                                              pairs[:, here, C:2 * C], ALU.add))
                c.wait()
                nc.gpsimd.tensor_tensor(tiles(gained[:])[:, here, :], tiles(centered[2][:])[:, here, :],
                                        g_rep[:].unsqueeze(1).broadcast_to([P, 8, C]),
                                        ALU.mult).then_inc(center_ready[2], 1)

            def iteration(i, cur, prev, nxt):
                f, g, n, pos = i, i - 1, i + 1, Places(i, cur, prev, nxt)
                if prev:
                    c = Chain(pool, ln2_p, g)
                    pool.wait_ge(rstd_ready[2], g + 1)
                    c.inc(nc.gpsimd.tensor_tensor(tiles(scaled[:]), tiles(gained[:]), per_tile(rstd[2]), ALU.mult))
                    c.wait()
                    nc.gpsimd.tensor_tensor(x2[:], scaled[:], x_tok[:, g % 2, :], ALU.add).then_inc(x2_ready, 1)
                    pool.wait_ge(x2_ready, g + 1)
                    center(3, x2[:], g)
                    scale(3, xhat3[:], g).then_inc(xhat_ready[3], 1)
                if nxt:
                    center(1, x_tok[:, n % 2, :], n)
                c = Chain(pool, heads_p, 8 * f)
                if cur:
                    sum_heads(pos, c, f, 0)
                    sum_heads(pos, c, f, 1)
                if nxt:
                    if cur:
                        pool.wait_ge(ek_used, KEXP * f + KEXP)
                    scale(1, xhat[:, :, 0:C], n).then_inc(xhat_ready[1], 1)
                if cur:
                    sum_heads(pos, c, f, 2)
                    sum_heads(pos, c, f, 3)

            run(pool, iteration)

        @block.scalar
        def _(act):
            act.wait_ge(setup_v, SETUP_V)

            def square(k, b):
                act.wait_ge(center_ready[k], 4 * b + 4 if k == 2 else b + 1)
                nc.scalar.activation(squares[k][:], centered[k][:], ACT.Square).then_inc(square_ready[k], 1)

            def copy_stack(k, pos, off):
                for u in range(STACK):
                    act.wait_ge(narrow_full, pos.n + off + u + 1)
                    nc.scalar.copy(stack[k][:, 1024 * u:1024 * u + 1024],
                                   narrow[:, (off + u) % 2, :].bitcast(f16)).then_inc(narrow_free, 1)

            def key_exp(pos, f, units):
                for u in units:
                    act.wait_ge(narrow_full, pos.n + pos.kexp + u + 1)
                    if not (isinstance(f, int) and KEXP * f + u < 2):
                        act.wait_ge(ek_used, KEXP * f + u - 1)
                    nc.scalar.activation(ek[:, u % 2, :, :].rearrange("p a b -> p (a b)"),
                                         narrow[:, (pos.kexp + u) % 2, :], ACT.Exp,
                                         scale=wscale[:, 0:1]).then_inc(narrow_free, 1)

            def iteration(i, cur, prev, nxt):
                f, g, n, pos = i, i - 1, i + 1, Places(i, cur, prev, nxt)
                if prev:
                    square(2, g)
                if cur:
                    copy_stack(1, pos, pos.stack1)
                    key_exp(pos, f, range(0, 6))
                if prev:
                    square(3, g)
                if cur:
                    key_exp(pos, f, range(6, KEXP))
                if nxt:
                    for u in range(XT):
                        act.wait_ge(narrow_full, pos.n + pos.xt + u + 1)
                        nc.scalar.copy(x_tok[:, n % 2, 512 * u:512 * u + 512],
                                       narrow[:, (pos.xt + u) % 2, :]).then_inc(narrow_free, 1)
                for step in STEPS:
                    if prev and step == AT_STACK3:
                        copy_stack(3, pos, pos.stack3)
                    if cur and step < QEXP:
                        u = step
                        act.wait_ge(narrow_full, pos.n + pos.qexp[u] + 1)
                        if u >= 2:
                            act.wait_ge(wide_full, pos.w + pos.norm[u - 2] + 1)
                        nc.scalar.activation(eq[:, u % 2, :], narrow[:, pos.qexp[u] % 2, :], ACT.Exp,
                                             scale=wscale[:, 0:1]).then_inc(narrow_free, 1)
                    if nxt and step == 0:
                        square(1, n)
                    if prev and step == LAG - 1:
                        act.wait_ge(gap_ready, g + 1)
                        nc.scalar.activation(e2[:], gap[:], ACT.Exp, scale=wscale[:, 2:3]).then_inc(e2_ready, 1)
                    if prev and step - LAG - 1 in (3, 7) or prev and step == STEPS[-1]:
                        u = (step - LAG - 1) // 4 if step < STEPS[-1] else 1
                        act.wait_ge(out_full, OUTU * g + u + 1)
                        if u == 0:
                            act.wait_ge(y_free, g + 1)
                        nc.scalar.copy(y_out[:, 512 * u:512 * u + 512],
                                       sums[:, :]).then_inc(y_ready, 1)

            run(act, iteration)

        @block.vector
        def _(dve):
            st = Chain(dve, setup_v, 0)
            dve.wait_ge(loaded, 16 * 15)
            dve.wait_ge(made, 21)
            for r in range(3):
                st.inc(nc.vector.tensor_copy(qk_nat[:, :, C * r:C * r + C], w_nat[:, 0:2, :]))
            for r in (96, 97):
                st.inc(nc.vector.tensor_copy(qk_nat[:, :, r:r + 1], b_nat[:, 0:2].unsqueeze(2)))
            st.inc(nc.vector.tensor_copy(v_nat[:, 0:C], w_nat[:, 2, :]))
            st.inc(nc.vector.tensor_copy(v_nat[:, C:C + 1], b_nat[:, 2:3]))
            st.inc(nc.vector.tensor_scalar(ctxscale[:], headmask[:], SCALE / N, None, ALU.mult))
            st.inc(nc.vector.tensor_reduce(bout_mean[:], bout_rep[:], AX.X, ALU.add, negate=True))
            st.wait()
            st.inc(nc.vector.tensor_scalar(bout_mean[:], bout_mean[:], 1.0 / C, None, ALU.mult))
            st.wait()
            st.inc(nc.vector.tensor_scalar(bout_centered[:], bout_rep[:], bout_mean[:], None, ALU.add))
            st.wait()
            st.inc(nc.vector.scalar_tensor_tensor(ctxbias[:], headmask[:], 1.0 / HEADS,
                                                  bout_centered[:].unsqueeze(1).broadcast_to([P, HEADS, C]),
                                                  ALU.mult, ALU.mult))
            st.inc(nc.vector.tensor_copy(mixz[:, P:P + HEADS], headmask[:, :, 0]))
            dve.wait_ge(setup_t, 1)
            st.inc(nc.vector.tensor_copy(w_rows[:, 0:2 * CH], wide[:, 0, 0:2 * CH]))
            st.inc(nc.vector.tensor_tensor(wo_block[:], headmask[:],
                                           wide[:, 0, 256:256 + C].unsqueeze(1).broadcast_to([P, HEADS, C]),
                                           ALU.mult))
            st.wait()
            for n, (lo, hi) in enumerate(groups):
                st.inc(nc.vector.tensor_reduce(amax[:, n:n + 1], w_rows[:, lo:hi], AX.X, ALU.max,
                                               apply_absolute_value=True))
            dve.wait_ge(setup_t, 2)
            st.inc(nc.vector.tensor_reduce(gmax[:], wide[0:3, 1, 0:P], AX.X, ALU.max))
            u_psum = wide[0:C + 1, 1, 512:512 + P].rearrange("p (h o) -> p h o", h=HEADS)
            st.inc(nc.vector.tensor_reduce(u_mean[:], u_psum, AX.X, ALU.add, negate=True))
            st.wait()
            st.inc(nc.vector.tensor_scalar(u_mean[:], u_mean[:], 1.0 / C, None, ALU.mult))
            st.wait()
            st.inc(nc.vector.tensor_tensor(u_mat[:].rearrange("p (h o) -> p h o", h=HEADS), u_psum,
                                           u_mean[:].unsqueeze(2).broadcast_to([C + 1, HEADS, C]), ALU.add))
            st.inc(nc.vector.tensor_scalar(gmax[:], gmax[:], 1e-30, None, ALU.max))
            st.wait()
            st.inc(nc.vector.tensor_scalar(gpow[:].bitcast(u32), gmax[:].bitcast(u32), 0x7F800000, None,
                                           ALU.bitwise_and))
            st.wait()
            st.inc(nc.vector.tensor_scalar(gdiag[:], ident[0:3, 0:3], gpow[:], None, ALU.mult))
            dve.wait_ge(setup_t, 3)
            st.inc(nc.vector.tensor_copy(wscale[:], wide[:, 0, 0:3]))
            st.wait()
            st.inc(nc.vector.reciprocal(winv[:], wscale[:]))
            st.wait()
            for n, (lo, hi) in enumerate(groups):
                st.inc(nc.vector.tensor_scalar(w_rows[:, lo:hi], w_rows[:, lo:hi], winv[:, n:n + 1], None, ALU.mult))
            st.wait()
            st.inc(nc.vector.tensor_copy(w_high[:], w_rows[:]))
            st.wait()
            st.inc(nc.vector.tensor_tensor(w_low[:], w_rows[:], w_high[:], ALU.subtract))
            st.wait()
            st.inc(nc.vector.tensor_scalar(w_high[:], w_high[:], row_high[:], None, ALU.mult))
            st.wait()
            st.inc(nc.vector.scalar_tensor_tensor(w_stack[:], w_low[:], row_low[:], w_high[:], ALU.mult, ALU.add))
            st.wait()
            assert st.n == SETUP_V, st.n

            def tiles(flat):
                return flat.rearrange("p (g c) -> p g c", c=C)

            def over_experts(stat):
                return stat[:].unsqueeze(2).broadcast_to([P, G, E])

            def mean(k, c, src):
                c.inc(nc.vector.tensor_reduce(nsum[k][:], tiles(src), AX.X, ALU.add, negate=True))
                c.wait()
                nc.vector.tensor_scalar(nmean[k][:], nsum[k][:], 1.0 / C, None, ALU.mult).then_inc(mean_ready[k], 1)

            def inverse_root(k, c, b, eps):
                dve.wait_ge(square_ready[k], b + 1)
                c.inc(nc.vector.tensor_reduce(vsum[k][:], tiles(squares[k][:]), AX.X, ALU.add))
                c.wait()
                c.inc(nc.vector.tensor_scalar(vari[k][:], vsum[k][:], 1.0 / C, eps, ALU.mult, ALU.add))
                c.wait()
                c.inc(nc.vector.tensor_scalar(root[k][:].bitcast(i32), vari[k][:].bitcast(i32), -0.5,
                                              float(0x5F3759DF), ALU.mult, ALU.add))
                c.wait()
                for n in range(3):
                    c.inc(nc.vector.tensor_tensor(rr[k][:], root[k][:], root[k][:], ALU.mult))
                    c.wait()
                    c.inc(nc.vector.scalar_tensor_tensor(ru[k][:], rr[k][:], -0.5, vari[k][:], ALU.mult, ALU.mult))
                    c.wait()
                    if n < 2:
                        c.inc(nc.vector.scalar_tensor_tensor(root[k][:], ru[k][:], 1.5, root[k][:], ALU.add, ALU.mult))
                        c.wait()
                nc.vector.scalar_tensor_tensor(rstd[k][:], ru[k][:], 1.5, root[k][:], ALU.add,
                                               ALU.mult).then_inc(rstd_ready[k], 1)

            def split(k, c, b, src):
                dve.wait_ge(xhat_ready[k], b + 1)
                c.inc(nc.vector.tensor_copy(parts[k][:, :, 0:C], src))
                nc.vector.tensor_copy(parts[k][:, :, 2 * C:3 * C], src).then_inc(parts_ready[k], 1)
                c.wait()
                nc.vector.tensor_tensor(parts[k][:, :, C:2 * C], src, parts[k][:, :, 0:C],
                                        ALU.subtract).then_inc(parts_ready[k], 1)

            def query_max(pos, c, g):
                for u in range(QMAX):
                    dve.wait_ge(wide_full, pos.w + pos.qmax + u + 1)
                    half = u // 2
                    nc.vector.tensor_reduce(nqmax[:, half, 32 * (u % 2):32 * (u % 2) + 32],
                                            wide[:, (pos.qmax + u) % 2, :].rearrange("p (a d) -> p a d", d=DH),
                                            AX.X, ALU.max, negate=True).then_inc(wide_free, 1)
                    if u % 2:
                        dve.wait_ge(wide_free, pos.w + pos.qmax + u + 1)
                        c.inc(nc.vector.tensor_copy(qmax_nat[:, half, 0, :], nqmax[:, half, :]))
                        c.wait()
                        nc.vector.tensor_tensor(qmax_nat[:, half, 1, :], nqmax[:, half, :], qmax_nat[:, half, 0, :],
                                                ALU.subtract).then_inc(qmax_nat_ready, 1)

            def copy_query_max(pos):
                for half in range(2):
                    dve.wait_ge(small_full, pos.s + pos.qtr + half + 1)
                    nc.vector.tensor_copy(qmax_tr[:, half, :],
                                          small[:, 0:P // 2].bitcast(f16)).then_inc(small_free, 1)

            def normalise(pos, c, units):
                for u in units:
                    dve.wait_ge(wide_full, pos.w + pos.norm[u] + 1)
                    src = wide[:, pos.norm[u] % 2, :].rearrange("p (t c) -> p t c", t=4)
                    c.inc(nc.vector.reciprocal(zrec[:, u % 2, :, :], src[:, :, P:P + HEADS]))
                    c.wait()
                    nc.vector.tensor_tensor(
                        heads[:, 4 * u:4 * u + 4, :].rearrange("p t (h c) -> p t h c", h=HEADS),
                        src[:, :, 0:P].rearrange("p t (h c) -> p t h c", h=HEADS),
                        zrec[:, u % 2, :, :].unsqueeze(3).broadcast_to([P, 4, HEADS, C]),
                        ALU.mult).then_inc(wide_free, 1)

            def key_max(pos, c):
                for u in range(KMAX):
                    dve.wait_ge(wide_full, pos.w + pos.kmax + u + 1)
                    nc.vector.tensor_reduce(kmax[:, u:u + 1], wide[:, (pos.kmax + u) % 2, :], AX.X,
                                            ALU.max).then_inc(wide_free, 1)
                dve.wait_ge(wide_free, pos.w + pos.kmax + KMAX)
                c.inc(nc.vector.tensor_reduce(nkmax[:], kmax[:], AX.X, ALU.max, negate=True))
                c.wait()
                c.inc(nc.vector.tensor_copy(kmax_nat[:, 98:99], nkmax[:]))
                c.wait()
                nc.vector.tensor_tensor(kmax_nat[:, 99:100], nkmax[:], kmax_nat[:, 98:99],
                                        ALU.subtract).then_inc(kmax_nat_ready, 1)

            def weights_with_key_max(pos):
                dve.wait_ge(small_full, pos.s + pos.ktr + 1)
                nc.vector.tensor_tensor(ws_kmax[:], ws_k, small[:, 0:P // 2].bitcast(f16),
                                        ALU.add).then_inc(small_free, 1)

            def context(pos, c, f):
                dve.wait_ge(ek_used, KEXP * f + KEXP)
                c.inc(nc.vector.reciprocal(grec[:], sums[:, C:C + 1]))
                c.wait()
                nc.vector.tensor_scalar(gnat[:, 0:C + 1], sums[:, 0:C + 1], grec[:], None, ALU.mult).then_inc(ctx_free, 1)
                dve.wait_ge(small_full, pos.s + pos.gtr + 1)
                nc.vector.tensor_copy(gtr[:], small[0:C + 1, 0:P]).then_inc(small_free, 1)
                dve.wait_ge(small_full, pos.s + pos.mix + 1)
                nc.vector.tensor_tensor(mix[:], small[:, 0:P], ctxscale[:].rearrange("p h c -> p (h c)"),
                                        ALU.mult).then_inc(small_free, 1)
                dve.wait_ge(small_free, pos.s + pos.mix + 1)
                nc.vector.tensor_tensor(mixz[:, 0:P], mix[:], ctxbias[:].rearrange("p h c -> p (h c)"),
                                        ALU.add).then_inc(mixz_ready, 1)

            def route(pos, c):
                dve.wait_ge(small_full, pos.s + pos.logit + 1)
                nc.vector.tensor_copy(logit[:].rearrange("p g e -> p (g e)"), small[:, 0:G * E]).then_inc(small_free, 1)
                dve.wait_ge(small_free, pos.s + pos.logit + 1)

                def step(ins):
                    c.inc(ins)
                    c.wait()

                step(nc.vector.tensor_reduce(top1[:], logit[:], AX.X, ALU.max))
                step(nc.vector.tensor_tensor(tie1[:], logit[:], over_experts(top1), ALU.is_equal))
                step(nc.vector.tensor_tensor(tie1[:], tie1[:], rank[:], ALU.mult))
                step(nc.vector.tensor_reduce(pick1[:], tie1[:], AX.X, ALU.max))
                step(nc.vector.tensor_tensor(one1[:], tie1[:], over_experts(pick1), ALU.is_equal))
                step(nc.vector.scalar_tensor_tensor(logit2[:].rearrange("p g e -> p (g e)"),
                                                    one1[:].rearrange("p g e -> p (g e)"), -3.0e38,
                                                    logit[:].rearrange("p g e -> p (g e)"), ALU.mult, ALU.add))
                step(nc.vector.tensor_reduce(top2[:], logit2[:], AX.X, ALU.max))
                nc.vector.tensor_tensor(gap[:], top2[:], top1[:], ALU.subtract).then_inc(gap_ready, 1)
                step(nc.vector.tensor_tensor(tie2[:], logit2[:], over_experts(top2), ALU.is_equal))
                step(nc.vector.tensor_tensor(tie2[:], tie2[:], rank[:], ALU.mult))
                step(nc.vector.tensor_reduce(pick2[:], tie2[:], AX.X, ALU.max))
                step(nc.vector.tensor_tensor(one2[:], tie2[:], over_experts(pick2), ALU.is_equal))

            def make_gates(c, h):
                def step(ins):
                    c.inc(ins)
                    c.wait()

                dve.wait_ge(e2_ready, h + 1)
                step(nc.vector.tensor_scalar(den[:], e2[:], 1.0, None, ALU.add))
                step(nc.vector.reciprocal(g1[:], den[:]))
                step(nc.vector.tensor_scalar(g1[:], g1[:], wscale[:, 1:2], None, ALU.mult))
                step(nc.vector.tensor_tensor(g2[:], g1[:], e2[:], ALU.mult))
                step(nc.vector.tensor_tensor(one1[:], one1[:], over_experts(g1), ALU.mult))
                step(nc.vector.tensor_tensor(one2[:], one2[:], over_experts(g2), ALU.mult))
                step(nc.vector.tensor_tensor(gates[:], one1[:], one2[:], ALU.add))

            def gate(pos, g, u):
                dve.wait_ge(wide_full, pos.w + pos.gate[u] + 1)
                if u >= 2:
                    dve.wait_ge(gated_used, GATE * g + u - 1)
                nc.vector.tensor_tensor(
                    gated[:, u % 2, :, :, :].rearrange("p e t c -> p t e c"),
                    wide[:, pos.gate[u] % 2, :].rearrange("p (t e c) -> p t e c", t=4, e=E),
                    gates[:, 4 * u:4 * u + 4, :].unsqueeze(3).broadcast_to([P, 4, E, C]),
                    ALU.mult).then_inc(wide_free, 1)

            def iteration(i, cur, prev, nxt):
                f, g, n, pos = i, i - 1, i + 1, Places(i, cur, prev, nxt)
                c1, ckq = Chain(dve, ln1_v, LN1_V * n), Chain(dve, kq_v, KQ_V * f)
                c23, cr = Chain(dve, ln23_v, LN23_V * g), Chain(dve, route_v, ROUTE_V * g)
                if prev:
                    inverse_root(2, c23, g, EPS)
                if cur:
                    key_max(pos, ckq)
                    query_max(pos, ckq, f)
                    weights_with_key_max(pos)
                    copy_query_max(pos)
                if prev:
                    dve.wait_ge(x2_ready, g + 1)
                    mean(3, c23, x2[:])
                    inverse_root(3, c23, g, EPS)
                if cur:
                    context(pos, ckq, f)
                if nxt:
                    dve.wait_ge(narrow_free, pos.n + pos.xt + XT)
                    mean(1, c1, x_tok[:, n % 2, :])
                if prev:
                    split(3, c23, g, xhat3[:])
                    assert c23.n == LN23_V, c23.n
                for step in STEPS:
                    if cur and 0 <= step - 1 < NORM:
                        normalise(pos, ckq, (step - 1,))
                    if nxt and step == 2:
                        inverse_root(1, c1, n, EPS_IN)
                    if prev and step == AT_ROUTE:
                        route(pos, cr)
                    if prev and step == LAG:
                        make_gates(cr, g)
                    if prev and 0 <= step - LAG < GATE:
                        gate(pos, g, step - LAG)
                    if nxt and step == LAG + 4:
                        split(1, c1, n, xhat[:, :, 0:C])
                if nxt:
                    assert c1.n == LN1_V, c1.n
                if cur:
                    assert ckq.n == KQ_V, ckq.n
                if prev:
                    assert cr.n == ROUTE_V, cr.n

            run(dve, iteration)

        @block.tensor
        def _(pe):
            def mm(dst, lhs, rhs, start=True, stop=True):
                return nc.tensor.matmul(dst, lhs, rhs, start=start, stop=stop)

            def tr(dst, src, idt, start=True, stop=True):
                return nc.tensor.matmul(dst, src, idt, is_transpose=True, start=start, stop=stop)

            pe.wait_ge(made, 11)
            pe.wait_ge(setup_v, 7)
            for s in range(2):
                tr(wide[:, 0, P * s:P * s + P], qk_nat[:, s, :], ident[:])
            tr(wide[:, 0, 256:256 + C], wo_nat[:, :], ident[0:C, 0:C]).then_inc(setup_t, 1)
            pe.wait_ge(setup_v, 18)
            tr(wide[0:3, 1, 0:P], amax[:, :], ident[:])
            mm(wide[0:C + 1, 1, 512:512 + P], v_nat[:, :],
               wo_block[:].rearrange("p h c -> p (h c)")).then_inc(setup_t, 1)
            pe.wait_ge(setup_v, 25)
            mm(wide[:, 0, 0:3], ones[0:3, :], gdiag[:, :]).then_inc(setup_t, 1)
            pe.wait_ge(setup_v, SETUP_V)

            def to_tokens(pos, f):
                pe.wait_ge(x_loaded, 16 * f + 16)
                for u in range(XT):
                    wait_slot(pe, narrow_free, pos.n + pos.xt + u, 2)
                    for t in range(4):
                        ins = tr(narrow[:, (pos.xt + u) % 2, P * t:P * t + P],
                                 x_in[:, 512 * u + P * t:512 * u + P * t + P], ident[:])
                    ins.then_inc(narrow_full, 1)

            def query_logits_by_token(pos):
                for u in range(QMAX):
                    wait_slot(pe, wide_free, pos.w + pos.qmax + u, 2)
                    for t in range(8):
                        tile = P * (8 * u + t)
                        ins = mm(wide[:, (pos.qmax + u) % 2, P * t:P * t + P], stack[1][:, tile:tile + P], ws_q)
                    ins.then_inc(wide_full, 1)

            def query_max_rows(pos, g):
                for half in range(2):
                    pe.wait_ge(qmax_nat_ready, 2 * g + half + 1)
                    wait_slot(pe, small_free, pos.s + pos.qtr + half, 1)
                    tr(small[:, 0:P // 2].bitcast(f16),
                       qmax_nat[:, half, :, :].rearrange("p a b -> p (a b)"), ident16[:]).then_inc(small_full, 1)

            def attend(pos, u):
                pe.wait_ge(narrow_free, pos.n + pos.qexp[u] + 1)
                wait_slot(pe, wide_free, pos.w + pos.norm[u], 2)
                for t in range(4):
                    ins = mm(wide[:, pos.norm[u] % 2, 256 * t:256 * t + P + HEADS],
                             eq[:, u % 2, P * t:P * t + P], mixz[:, :])
                ins.then_inc(wide_full, 1)

            def query_logits(pos, u):
                half = u // 4
                wait_slot(pe, narrow_free, pos.n + pos.qexp[u], 2)
                pe.wait_ge(small_free, pos.s + pos.qtr + half + 1)
                slot = pos.qexp[u] % 2
                mm(narrow[:, slot, :], ws_q, stack[1][:, 512 * u:512 * u + 512], stop=False)
                for t in range(4):
                    ins = mm(narrow[:, slot, P * t:P * t + P], maxpick[:, 4 * (u % 4) + t, :],
                             qmax_tr[:, half, :], start=False, stop=(t == 3))
                ins.then_inc(narrow_full, 1)

            def make_stack(k, pos, off, b):
                pe.wait_ge(parts_ready[k], 2 * b + 2)
                for u in range(STACK):
                    wait_slot(pe, narrow_free, pos.n + off + u, 2)
                    for t in range(8):
                        ins = tr(narrow[:, (off + u) % 2, P // 2 * t:P // 2 * t + P // 2].bitcast(f16),
                                 parts[k][:, 8 * u + t, :], ident16[:])
                    ins.then_inc(narrow_full, 1)

            def key_logits_by_channel(pos):
                for u in range(KMAX):
                    pe.wait_ge(narrow_free, pos.n + pos.stack1 + u + 1)
                    wait_slot(pe, wide_free, pos.w + pos.kmax + u, 2)
                    for h in range(2):
                        at = 1024 * u + 512 * h
                        ins = mm(wide[:, (pos.kmax + u) % 2, 512 * h:512 * h + 512], ws_k, stack[1][:, at:at + 512])
                    ins.then_inc(wide_full, 1)

            def sum_context(pos, u):
                pe.wait_ge(narrow_free, pos.n + pos.kexp + u + 1)
                for t in range(4):
                    ins = mm(sums[:, 0:C + 1], ek[:, u % 2, t, :], xhat[:, 4 * u + t, :],
                             start=(u == 0 and t == 0), stop=(u == KEXP - 1 and t == 3))
                ins.then_inc(ek_used, 1)

            def key_max_row(pos, f):
                pe.wait_ge(kmax_nat_ready, f + 1)
                wait_slot(pe, small_free, pos.s + pos.ktr, 1)
                tr(small[:, 0:P // 2].bitcast(f16), kmax_nat[:, :], ident16[:]).then_inc(small_full, 1)

            def key_side(pos, f, first, tail_before):
                pe.wait_ge(small_free, pos.s + pos.ktr + 1)
                if tail_before:
                    pe.wait_ge(y_ready, OUTU * (f - 1))
                if not first:
                    pe.wait_ge(ctx_free, f)
                for u in range(KEXP):
                    wait_slot(pe, narrow_free, pos.n + pos.kexp + u, 2)
                    for t in range(4):
                        tile = P * (4 * u + t)
                        ins = mm(narrow[:, (pos.kexp + u) % 2, P * t:P * t + P], stack[1][:, tile:tile + P], ws_kmax[:])
                    ins.then_inc(narrow_full, 1)
                    if u:
                        sum_context(pos, u - 1)
                sum_context(pos, KEXP - 1)
                pe.wait_ge(ctx_free, f + 1)
                wait_slot(pe, small_free, pos.s + pos.gtr, 1)
                tr(small[:, 0:P], gnat[:, :], ident[:]).then_inc(small_full, 1)
                pe.wait_ge(small_free, pos.s + pos.gtr + 1)
                mm(small[:, 0:P], gtr[:, :], u_mat[:, :]).then_inc(small_full, 1)

            def router(pos):
                pe.wait_ge(narrow_free, pos.n + pos.stack3 + STACK)
                wait_slot(pe, small_free, pos.s + pos.logit, 1)
                for t in range(G):
                    ins = mm(small[:, E * t:E * t + E], stack[3][:, P * t:P * t + P], ws_r)
                ins.then_inc(small_full, 1)

            def experts(pos, u):
                wait_slot(pe, wide_free, pos.w + pos.gate[u], 2)
                for t in range(4):
                    tile = P * (4 * u + t)
                    ins = mm(wide[:, pos.gate[u] % 2, 256 * t:256 * t + 256], stack[3][:, tile:tile + P], ws_e)
                ins.then_inc(wide_full, 1)

            def add_experts(pos, g, v):
                pe.wait_ge(wide_free, pos.w + pos.gate[v] + 1)
                if v % 4 == 0:
                    if not (isinstance(g, int) and g == 0 and v == 0):
                        pe.wait_ge(y_ready, OUTU * g + v // 4)
                dst = sums[:, P * (v % 4):P * (v % 4) + P]
                for e in range(E):
                    ins = tr(dst, gated[:, v % 2, e, :, :].rearrange("p t c -> p (t c)"), ident[:], start=(e == 0), stop=False)
                ins.then_inc(gated_used, 1)
                ins = tr(dst, x2[:, P * v:P * v + P], ident[:], start=False, stop=True)
                if v % 4 == 3:
                    ins.then_inc(out_full, 1)

            def iteration(i, cur, prev, nxt):
                f, g, n, pos = i, i - 1, i + 1, Places(i, cur, prev, nxt)
                if cur:
                    make_stack(1, pos, pos.stack1, f)
                    key_logits_by_channel(pos)
                    query_logits_by_token(pos)
                    key_max_row(pos, f)
                    query_max_rows(pos, f)
                    key_side(pos, f, isinstance(f, int) and f == 0, not isinstance(f, int) or f > 1)
                if nxt:
                    to_tokens(pos, n)
                for step in STEPS:
                    if prev and step == AT_STACK3:
                        make_stack(3, pos, pos.stack3, g)
                    if cur and step < QEXP:
                        query_logits(pos, step)
                    if prev and step == AT_ROUTE:
                        router(pos)
                    if cur and 0 <= step - 1 < NORM:
                        if step == 1:
                            pe.wait_ge(mixz_ready, f + 1)
                        attend(pos, step - 1)
                    if prev and 0 <= step - LAG < GATE:
                        experts(pos, step - LAG)
                    if prev and 0 <= step - LAG - 1 < GATE:
                        add_experts(pos, g, step - LAG - 1)
                if prev:
                    add_experts(pos, g, GATE - 1)

            run(pe, iteration)


_INS = ['x', 'L0_conv_w_qkv', 'L0_conv_b_qkv', 'L0_conv_w_out', 'L0_conv_b_out', 'L0_conv_g_ln',
        'L0_ffn_router_w', 'L0_ffn_router_b', 'L0_ffn_expert_w', 'L0_ffn_expert_b']


def kernel(**inputs):
    import numpy as _np
    import concourse.bacc as _bacc
    from concourse import mybir as _mybir
    from concourse.bass_utils import run_bass_kernel_spmd as _run
    nc = _bacc.Bacc("TRN2", target_bir_lowering=False, num_devices=1)
    arrays, args = {}, []
    for name in _INS:
        a = _np.ascontiguousarray(inputs[name])
        arrays[f"in_{name}_dram"] = a
        args.append(nc.dram_tensor(f"in_{name}_dram", a.shape, _mybir.dt.from_np(a.dtype), kind="ExternalInput").ap())
    out = nc.dram_tensor("out_dram", (8, 32, 64, 64), _mybir.dt.float32, kind="ExternalOutput").ap()
    build(nc, *args, out)
    r = _run(nc, [arrays], core_ids=[0])
    return r.results[0]["out_dram"]
```

```python
import concourse.bass as bass
from concourse import mybir
from contextlib import ExitStack

NB, C, N = 8, 32, 4096
HEADS, DH = 4, 32
CH = HEADS * DH
P = 128
G = N // P
J = P // C
T = G // J
E = 8
EPS = 1e-5
EPS_IN = 1e-6
SCALE = DH ** -0.5

QMAX, NORM, KMAX, GATE = 4, 8, 4, 8
XT, STACK, KEXP = 2, 4, 8
OUTU = 2
LAST = 26
STEPS = range(LAST)
AT_QEXP = (0, 0, 1, 1, 2, 3, 4, 5)
AT_ATTEND = (1, 2, 3, 4, 5, 5, 6, 7)
AT_HEADS = (2, 4, 6, 8)
AT_SQUARE2 = 10
AT_X2 = 13
AT_CENTER3 = 15
AT_SCALE3 = 21
AT_RSTD2 = (10, 11, 11, 12)
AT_MEAN3 = 15
AT_SQUARE3 = 18
AT_RSTD3 = (19, 19, 20, 20)
AT_SPLIT3 = 22
AT_STACK3 = (1, 1, 2, 3)
AT_ROUTER = 4
AT_ROUTE = (4, 5, 6, 7, 7, 8)
AT_RESIDUAL = 6
AT_E2 = 9
AT_GATES = 9
AT_EXPERTS = (11, 11, 12, 13, 14, 16, 18, 20)
AT_OUT = (11, 12, 13, 14, 15, 17, 19, 21)
AT_XT = (19, 19)
AT_MEAN1 = 20
AT_CENTER1 = 20
AT_SQUARE1 = 21
AT_RSTD1 = (22, 23, 23, 24)
AT_SCALE1 = 2
AT_SPLIT1 = 3
AT_STACK1 = (6, 6, 7, 8)
AT_KMAX = (7, 8, 9, 10)
AT_KROW = 11
AT_KROW_TURN = 12
AT_KROW_ADD = 12
AT_QMAX = (13, 14, 15, 16)
AT_QROWS = (17, 18)
AT_KEXP = (13, 14, 15, 16, 17, 18, 19, 20)
AT_SUMS = (14, 15, 16, 17, 18, 19, 20, 20)
AT_CONTEXT = (21, 22)
AT_MIX = 22
EKS, EQS = 4, 8
GATEDS = 4
SETUP_V = 35


def build(nc, x, w_qkv, b_qkv, w_out, b_out, g_ln, router_w, router_b, expert_w, expert_b, out):
    f32, f16, u32, i32 = mybir.dt.float32, mybir.dt.float16, mybir.dt.uint32, mybir.dt.int32
    ALU, ACT, AX = mybir.AluOpType, mybir.ActivationFunctionType, mybir.AxisListType
    x_v = x.rearrange("b c (j t) f -> b j c (t f)", j=J)
    out_v = out.rearrange("b c (j t) f -> b j c (t f)", j=J)

    ctx = ExitStack()
    with ctx:
        def sb(name, shape, dt=f32):
            return ctx.enter_context(nc.sbuf_tensor(name, shape, dt))

        def sem(name):
            return ctx.enter_context(nc.semaphore(name))

        ident = sb("ident", [P, P])
        ident16 = sb("ident16", [P, P], f16)
        ones = sb("ones", [P, P])
        headmask = sb("headmask", [P, HEADS, C])
        ctxscale = sb("ctxscale", [P, HEADS, C])
        ctxbias = sb("ctxbias", [P, HEADS, C])
        bout_rep = sb("bout_rep", [P, C])
        bout_mean = sb("bout_mean", [P, 1])
        bout_centered = sb("bout_centered", [P, C])
        g_rep = sb("g_rep", [P, C])
        u_mean = sb("u_mean", [C + 1, HEADS])
        maxpick = sb("maxpick", [P, 16, CH], f16)
        rank = sb("rank", [P, G, E])
        row_high = sb("row_high", [P, 1])
        row_low = sb("row_low", [P, 1])
        w_nat = sb("w_nat", [P, 3, C])
        b_nat = sb("b_nat", [P, 3])
        qk_nat = sb("qk_nat", [P, 2, P])
        v_nat = sb("v_nat", [P, C + 1])
        wo_nat = sb("wo_nat", [C, P])
        wo_block = sb("wo_block", [P, HEADS, C])
        u_mat = sb("u_mat", [C + 1, P + 1])
        NW = 2 * CH + E * C + E
        w_rows = sb("w_rows", [P, NW])
        w_high = sb("w_high", [P, NW], f16)
        w_low = sb("w_low", [P, NW], f16)
        w_stack = sb("w_stack", [P, NW], f16)
        groups = [(0, 2 * CH), (2 * CH, 2 * CH + E * C), (2 * CH + E * C, NW)]
        amax = sb("amax", [P, 3])
        gmax = sb("gmax", [3, 1])
        gpow = sb("gpow", [3, 1])
        gdiag = sb("gdiag", [3, 3])
        wscale = sb("wscale", [P, 3])
        winv = sb("winv", [P, 3])
        ws_q = w_stack[:, 0:CH]
        ws_k = w_stack[:, CH:2 * CH]
        ws_e = w_stack[:, 2 * CH:2 * CH + E * C]
        ws_r = w_stack[:, 2 * CH + E * C:NW]
        x_in = sb("x_in", [P, N // J])
        x_tok = sb("x_tok", [P, 2, G * C])
        LN = (1, 2, 3)
        centered = {k: sb(f"centered{k}", [P, G * C]) for k in LN}
        squares = {k: sb(f"squares{k}", [P, G * C]) for k in LN}
        nsum = {k: sb(f"nsum{k}", [P, G]) for k in (1, 3)}
        nmean = {k: sb(f"nmean{k}", [P, G]) for k in (1, 3)}
        vsum = {k: sb(f"vsum{k}", [P, G]) for k in LN}
        vari = {k: sb(f"vari{k}", [P, G]) for k in LN}
        root = {k: sb(f"root{k}", [P, G]) for k in LN}
        rr = {k: sb(f"rr{k}", [P, G]) for k in LN}
        ru = {k: sb(f"ru{k}", [P, G]) for k in LN}
        rstd = {k: sb(f"rstd{k}", [P, G]) for k in LN}
        xhat = sb("xhat", [P, G, C + 1])
        xhat3 = sb("xhat3", [P, G, C])
        parts = {k: sb(f"parts{k}", [P, G, P], f16) for k in (1, 3)}
        stack = {k: sb(f"stack{k}", [P, N], f16) for k in (1, 3)}
        kmax = sb("kmax", [P, KMAX])
        nkmax = sb("nkmax", [P, 1])
        kmax_nat = sb("kmax_nat", [P, P], f16)
        ws_kmax = sb("ws_kmax", [P, CH], f16)
        ek = sb("ek", [P, EKS, 4, CH])
        sums_ctx = sb("sums_ctx", [C + 1, P])
        grec = sb("grec", [P, 1])
        mix = sb("mix", [P, P])
        mixz = sb("mixz", [P, P + HEADS])
        nqmax = sb("nqmax", [P, 2, 16 * HEADS])
        qmax_nat = sb("qmax_nat", [P, 2, 2, 16 * HEADS], f16)
        qmax_tr = sb("qmax_tr", [P, 2, P], f16)
        eq = sb("eq", [P, EQS, 4 * P])
        zrec = sb("zrec", [P, 2, 4, HEADS])
        heads = sb("heads", [P, G, CH])
        pairs = sb("pairs", [P, G, 2 * C])
        scaled = sb("scaled", [P, G * C])
        gained = sb("gained", [P, G * C])
        x2 = sb("x2", [P, G * C])
        residual = sb("residual", [P, G * C])
        logit = sb("logit", [P, G, E])
        logit2 = sb("logit2", [P, G, E])
        tie1 = sb("tie1", [P, G, E])
        tie2 = sb("tie2", [P, G, E])
        one1 = sb("one1", [P, G, E])
        one2 = sb("one2", [P, G, E])
        gates = sb("gates", [P, G, E])
        top1 = sb("top1", [P, G])
        top2 = sb("top2", [P, G])
        pick1 = sb("pick1", [P, G])
        pick2 = sb("pick2", [P, G])
        gap = sb("gap", [P, G])
        e2 = sb("e2", [P, G])
        den = sb("den", [P, G])
        g1 = sb("g1", [P, G])
        g2 = sb("g2", [P, G])
        gated = sb("gated", [P, GATEDS, E, 4, C])
        y_out = sb("y_out", [P, N // J])

        wide = ctx.enter_context(nc.psum_tensor("wide", [P, 2, 1024], f32))
        narrow = ctx.enter_context(nc.psum_tensor("narrow", [P, 2, 512], f32))
        sums = ctx.enter_context(nc.psum_tensor("sums", [P, 512], f32))
        small = ctx.enter_context(nc.psum_tensor("small", [P, 512], f32))

        loaded = sem("weights_loaded")
        made = sem("constants_made")
        setup_v = sem("setup_vector_steps")
        setup_t = sem("setup_tensor_steps")
        x_loaded = sem("x_loaded")
        stored = sem("stored")
        wide_full, wide_free = sem("wide_full"), sem("wide_free")
        narrow_full, narrow_free = sem("narrow_full"), sem("narrow_free")
        small_full, small_free = sem("small_full"), sem("small_free")
        mean_ready = {k: sem(f"mean_ready{k}") for k in (1, 3)}
        center_ready = {k: sem(f"center_ready{k}") for k in LN}
        square_ready = {k: sem(f"square_ready{k}") for k in LN}
        rstd_ready = {k: sem(f"rstd_ready{k}") for k in LN}
        xhat_ready = {k: sem(f"xhat_ready{k}") for k in (1, 3)}
        high_ready = {k: sem(f"high_ready{k}") for k in (1, 3)}
        parts_ready = {k: sem(f"parts_ready{k}") for k in (1, 3)}
        kmax_nat_ready = sem("kmax_nat_ready")
        ek_used = sem("ek_used")
        mixz_ready = sem("mixz_ready")
        qmax_nat_ready = sem("qmax_nat_ready")
        x2_ready = sem("x2_ready")
        residual_ready = sem("residual_ready")
        gap_ready, e2_ready = sem("gap_ready"), sem("e2_ready")
        probs_ready, gates_ready = sem("probs_ready"), sem("gates_ready")
        gated_used = sem("gated_used")
        out_full = sem("out_full")
        y_ready = sem("y_ready")
        y_free = sem("y_free")
        ln1_v, kq_v = sem("layernorm1_vector_steps"), sem("key_query_vector_steps")
        norm_v = sem("normalise_vector_steps")
        ln23_v, route_v = sem("layernorm23_vector_steps"), sem("route_vector_steps")
        heads_p, ln2_p, gates_p = sem("heads_pool_steps"), sem("layernorm2_pool_steps"), sem("gates_pool_steps")
        LN1_V, KQ_V, LN23_V, ROUTE_V = 10, 5, 19, 14

        class Chain:

            def __init__(self, eng, s, base):
                self.eng, self.s, self.base, self.n = eng, s, base, 0

            def inc(self, ins):
                ins.then_inc(self.s, 1)
                self.n += 1
                return self

            def wait(self):
                self.eng.wait_ge(self.s, self.base + self.n)

        class Places:

            def __init__(self, i, cur, prev, nxt, ahead):
                if isinstance(i, int):
                    a, b, c, d = (min(max(i + k, 0), NB) for k in (2, 1, 0, -1))
                    self.w, self.n, self.s = 8 * b + 8 * c + 8 * d, 2 * a + 14 * b + 8 * c + 4 * d, 3 * b + d
                else:
                    self.w, self.n, self.s = 24 * i, 28 * i + 14, 4 * i + 2
                w = n = s = 0
                self.qexp, self.norm, self.gate, self.kmax, self.qmax = {}, {}, {}, {}, {}
                self.xt, self.qrows, self.kexp, self.stack = {}, {}, {}, {1: {}, 3: {}}
                if prev:
                    self.logit, s = s, s + 1
                if nxt:
                    self.ktr, self.ctx, self.mix = s, s + 1, s + 2
                for step in STEPS:
                    for there, table, at in ((ahead, self.xt, AT_XT), (prev, self.stack[3], AT_STACK3),
                                             (cur, self.qexp, AT_QEXP), (nxt, self.stack[1], AT_STACK1),
                                             (nxt, self.kexp, AT_KEXP), (nxt, self.qrows, AT_QROWS)):
                        for unit, its_step in enumerate(at):
                            if there and its_step == step:
                                table[unit], n = n, n + 1
                    for there, table, at in ((cur, self.norm, AT_ATTEND), (prev, self.gate, AT_EXPERTS),
                                             (nxt, self.kmax, AT_KMAX), (nxt, self.qmax, AT_QMAX)):
                        for unit, its_step in enumerate(at):
                            if there and its_step == step:
                                table[unit], w = w, w + 1

        def run(engine, iteration, set_up=None):
            iteration(-2, False, False, False, True)
            if set_up:
                set_up()
            iteration(-1, False, False, True, True)
            iteration(0, True, False, True, True)
            with engine.Fori(1, NB - 2) as i:
                iteration(i, True, True, True, True)
            iteration(NB - 2, True, True, True, False)
            iteration(NB - 1, True, True, False, False)
            iteration(NB, False, True, False, False)

        def units(there, at, step):
            return [unit for unit, its_step in enumerate(at) if there and its_step == step]

        def wait_slot(eng, free, at, slots):
            if isinstance(at, int) and at < slots:
                return
            eng.wait_ge(free, at - slots + 1)

        block = ctx.enter_context(nc.Block())

        @block.sync
        def _(sp):
            def load(b):
                sp.dma_start(x_in[:, :], x_v[bass.ds(b, 1)].rearrange("b j c i -> (b j) c i")).then_inc(x_loaded, 16)

            load(0)
            sp.dma_start(w_nat[:, :, :], w_qkv.rearrange("(s p) c -> p s c", p=P)).then_inc(loaded, 16)
            sp.dma_start(b_nat[:, :], b_qkv.rearrange("(s p) -> p s", p=P),
                         allow_slow_non_contiguous=True).then_inc(loaded, 16)
            sp.dma_start(wo_nat[:, :], w_out).then_inc(loaded, 16)
            sp.dma_start(bout_rep[:, :], b_out.partition_broadcast(P)).then_inc(loaded, 16)
            sp.dma_start(g_rep[:, :], g_ln.partition_broadcast(P)).then_inc(loaded, 16)
            sp.wait_ge(made, 1)
            lo, hi = groups[1]
            for r in range(3):
                rows = slice(C * r, C * r + C)
                sp.dma_start(w_rows[rows, lo:hi].rearrange("d (e c) -> d e c", e=E),
                             expert_w.rearrange("e d c -> d e c")).then_inc(loaded, 16)
                sp.dma_start(w_rows[rows, hi:NW], router_w).then_inc(loaded, 16)
            for r in (96, 97):
                sp.dma_start(w_rows[r:r + 1, lo:hi],
                             expert_b.rearrange("e c -> (e c)").unsqueeze(0)).then_inc(loaded, 16)
                sp.dma_start(w_rows[r:r + 1, hi:NW], router_b.unsqueeze(0)).then_inc(loaded, 16)

            def store(b):
                sp.wait_ge(y_ready, OUTU * b + OUTU)
                sp.dma_start(out_v[bass.ds(b, 1)].rearrange("b j c i -> (b j) c i"), y_out[:, :]).then_inc(stored, 16)
                sp.wait_ge(stored, 16 * b + 16)
                sp.sem_inc(y_free, 1)

            def load_next(b):
                sp.wait_ge(mean_ready[1], b)
                load(b)

            sp.sem_inc(y_free, 1)
            load_next(1)
            load_next(2)
            with sp.Fori(1, NB - 2) as i:
                load_next(i + 2)
                store(i - 1)
            for b in range(NB - 3, NB):
                store(b)

        @block.gpsimd
        def _(pool):
            nc.gpsimd.memset(w_rows[:], 0.0).then_inc(made, 1)
            nc.gpsimd.memset(ones[:], 1.0).then_inc(made, 1)
            nc.gpsimd.memset(maxpick[:], 0.0).then_inc(made, 1)
            nc.gpsimd.memset(qk_nat[:], 0.0).then_inc(made, 1)
            nc.gpsimd.memset(kmax_nat[:], 0.0).then_inc(made, 1)
            nc.gpsimd.memset(xhat[:, :, C:C + 1], 1.0).then_inc(made, 1)
            for k in (1, 3):
                nc.gpsimd.memset(parts[k][:, :, 96:P], 1.0).then_inc(made, 1)
            pool.wait_ge(made, 8)
            nc.gpsimd.affine_select(out=ident[:], in_=ones[:], pattern=[[-1, P]], compare_op=ALU.is_equal,
                                    fill=0.0, base=0, channel_multiplier=1).then_inc(made, 1)
            nc.gpsimd.affine_select(out=ident16[:], in_=ones[:], pattern=[[-1, P]], compare_op=ALU.is_equal,
                                    fill=0.0, base=0, channel_multiplier=1).then_inc(made, 1)
            nc.gpsimd.affine_select(out=headmask[:], in_=ones[:].rearrange("p (h c) -> p h c", h=HEADS),
                                    pattern=[[-DH, HEADS], [0, C]], compare_op=ALU.is_ge,
                                    fill=0.0, base=0, channel_multiplier=1).then_inc(made, 1)
            nc.gpsimd.affine_select(out=maxpick[:].rearrange("p t (h d) -> p t h d", h=HEADS),
                                    in_=maxpick[:].rearrange("p t (h d) -> p t h d", h=HEADS),
                                    pattern=[[-HEADS, 16], [-1, HEADS], [0, DH]], compare_op=ALU.not_equal,
                                    fill=1.0, base=0, channel_multiplier=1).then_inc(made, 1)
            nc.gpsimd.affine_select(out=row_high[:], in_=ones[:, 0:1], pattern=[[0, 1]], compare_op=ALU.is_ge,
                                    fill=0.0, base=63, channel_multiplier=-1).then_inc(made, 1)
            nc.gpsimd.affine_select(out=row_low[:], in_=ones[:, 0:1], pattern=[[0, 1]], compare_op=ALU.is_ge,
                                    fill=0.0, base=-64, channel_multiplier=1).then_inc(made, 1)
            pool.wait_ge(made, 14)
            nc.gpsimd.affine_select(out=headmask[:], in_=headmask[:], pattern=[[DH, HEADS], [0, C]],
                                    compare_op=ALU.is_ge, fill=0.0, base=DH - 1,
                                    channel_multiplier=-1).then_inc(made, 1)
            nc.gpsimd.affine_select(out=maxpick[:].rearrange("p t (h d) -> p t h d", h=HEADS),
                                    in_=maxpick[:].rearrange("p t (h d) -> p t h d", h=HEADS),
                                    pattern=[[-HEADS, 16], [-1, HEADS], [0, DH]], compare_op=ALU.not_equal,
                                    fill=1.0, base=-64, channel_multiplier=1).then_inc(made, 1)
            nc.gpsimd.affine_select(out=row_high[:], in_=row_high[:], pattern=[[0, 1]], compare_op=ALU.not_equal,
                                    fill=1.0, base=-96, channel_multiplier=1).then_inc(made, 1)
            nc.gpsimd.affine_select(out=row_low[:], in_=row_low[:], pattern=[[0, 1]], compare_op=ALU.is_ge,
                                    fill=0.0, base=95, channel_multiplier=-1).then_inc(made, 1)
            pool.wait_ge(made, 18)
            nc.gpsimd.affine_select(out=row_low[:], in_=row_low[:], pattern=[[0, 1]], compare_op=ALU.not_equal,
                                    fill=1.0, base=-97, channel_multiplier=1).then_inc(made, 1)
            nc.gpsimd.iota(rank[:], pattern=[[0, G], [-1, E]], base=E, channel_multiplier=0,
                           allow_small_or_imprecise_dtypes=True).then_inc(made, 1)

            def per_tile(stat):
                return stat[:].unsqueeze(2).broadcast_to([P, G, C])

            def tiles(flat):
                return flat.rearrange("p (g c) -> p g c", c=C)

            def center(k, src, b):
                pool.wait_ge(mean_ready[k], b + 1)
                nc.gpsimd.tensor_tensor(tiles(centered[k][:]), tiles(src), per_tile(nmean[k]),
                                        ALU.add).then_inc(center_ready[k], 1)

            def scale(k, dst, b):
                pool.wait_ge(rstd_ready[k], b + 1)
                return nc.gpsimd.tensor_tensor(dst, tiles(centered[k][:]), per_tile(rstd[k]), ALU.mult)

            def over_experts(stat):
                return stat[:].unsqueeze(2).broadcast_to([P, G, E])

            def make_gates(c, g):
                pool.wait_ge(probs_ready, g + 1)
                c.inc(nc.gpsimd.tensor_tensor(one1[:], one1[:], over_experts(g1), ALU.mult))
                c.inc(nc.gpsimd.tensor_tensor(one2[:], one2[:], over_experts(g2), ALU.mult))
                c.wait()
                nc.gpsimd.tensor_tensor(gates[:], one1[:], one2[:], ALU.add).then_inc(gates_ready, 1)

            def sum_heads(pos, c, f, q):
                pool.wait_ge(wide_free, pos.w + pos.norm[2 * q + 1] + 1)
                here = slice(8 * q, 8 * q + 8)
                c.inc(nc.gpsimd.tensor_tensor(pairs[:, here, :], heads[:, here, 0:2 * C], heads[:, here, 2 * C:4 * C],
                                              ALU.add))
                c.wait()
                c.inc(nc.gpsimd.tensor_tensor(tiles(centered[2][:])[:, here, :], pairs[:, here, 0:C],
                                              pairs[:, here, C:2 * C], ALU.add))
                c.wait()
                nc.gpsimd.tensor_tensor(tiles(gained[:])[:, here, :], tiles(centered[2][:])[:, here, :],
                                        g_rep[:].unsqueeze(1).broadcast_to([P, 8, C]),
                                        ALU.mult).then_inc(center_ready[2], 1)

            def iteration(i, cur, prev, nxt, ahead):
                f, g, n, m, pos = i, i - 1, i + 1, i + 2, Places(i, cur, prev, nxt, ahead)
                ch, c2, cg = Chain(pool, heads_p, 8 * f), Chain(pool, ln2_p, f), Chain(pool, gates_p, 2 * g)
                for step in STEPS:
                    if prev and step == AT_GATES:
                        make_gates(cg, g)
                    if nxt and step == AT_SCALE1:
                        if cur:
                            pool.wait_ge(ek_used, KEXP * f + KEXP)
                        scale(1, xhat[:, :, 0:C], n).then_inc(xhat_ready[1], 1)
                    if cur and step in AT_HEADS:
                        sum_heads(pos, ch, f, AT_HEADS.index(step))
                    if cur and step == AT_X2:
                        pool.wait_ge(rstd_ready[2], f + 1)
                        c2.inc(nc.gpsimd.tensor_tensor(tiles(scaled[:]), tiles(gained[:]), per_tile(rstd[2]), ALU.mult))
                        c2.wait()
                        if prev:
                            pool.wait_ge(residual_ready, g + 1)
                        nc.gpsimd.tensor_tensor(x2[:], scaled[:], x_tok[:, f % 2, :], ALU.add).then_inc(x2_ready, 1)
                    if cur and step == AT_CENTER3:
                        pool.wait_ge(x2_ready, f + 1)
                        center(3, x2[:], f)
                    if ahead and step == AT_CENTER1:
                        center(1, x_tok[:, m % 2, :], m)
                    if cur and step == AT_SCALE3:
                        scale(3, xhat3[:], f).then_inc(xhat_ready[3], 1)

            run(pool, iteration)

        @block.scalar
        def _(act):
            def set_up():
                act.wait_ge(setup_v, SETUP_V)

            def square(k, b):
                act.wait_ge(center_ready[k], 4 * b + 4 if k == 2 else b + 1)
                nc.scalar.activation(squares[k][:], centered[k][:], ACT.Square).then_inc(square_ready[k], 1)

            def copy_stack(k, pos, u):
                act.wait_ge(narrow_full, pos.n + pos.stack[k][u] + 1)
                nc.scalar.copy(stack[k][:, 1024 * u:1024 * u + 1024],
                               narrow[:, pos.stack[k][u] % 2, :].bitcast(f16)).then_inc(narrow_free, 1)

            def high_parts(k, b, src):
                act.wait_ge(xhat_ready[k], b + 1)
                nc.scalar.copy(parts[k][:, :, 0:C], src).then_inc(high_ready[k], 1)
                nc.scalar.copy(parts[k][:, :, 2 * C:3 * C], src).then_inc(parts_ready[k], 1)

            def key_exp(pos, n, u):
                act.wait_ge(narrow_full, pos.n + pos.kexp[u] + 1)
                if not (isinstance(n, int) and KEXP * n + u < EKS):
                    act.wait_ge(ek_used, KEXP * n + u - EKS + 1)
                nc.scalar.activation(ek[:, u % EKS, :, :].rearrange("p a b -> p (a b)"),
                                     narrow[:, pos.kexp[u] % 2, :], ACT.Exp,
                                     scale=wscale[:, 0:1]).then_inc(narrow_free, 1)

            def query_exp(pos, f, u):
                act.wait_ge(narrow_full, pos.n + pos.qexp[u] + 1)
                if u == 0 and not (isinstance(f, int) and f == 0):
                    act.wait_ge(wide_full, pos.w)
                nc.scalar.activation(eq[:, u % EQS, :], narrow[:, pos.qexp[u] % 2, :], ACT.Exp,
                                     scale=wscale[:, 0:1]).then_inc(narrow_free, 1)

            def copy_output(g, u):
                act.wait_ge(out_full, OUTU * g + u + 1)
                if u == 0:
                    act.wait_ge(y_free, g + 1)
                nc.scalar.copy(y_out[:, 512 * u:512 * u + 512], sums[:, :]).then_inc(y_ready, 1)

            def iteration(i, cur, prev, nxt, ahead):
                f, g, n, m, pos = i, i - 1, i + 1, i + 2, Places(i, cur, prev, nxt, ahead)
                for step in STEPS:
                    for u in units(ahead, AT_XT, step):
                        act.wait_ge(narrow_full, pos.n + pos.xt[u] + 1)
                        if cur and u == 0:
                            act.wait_ge(x2_ready, f + 1)
                        nc.scalar.copy(x_tok[:, m % 2, 512 * u:512 * u + 512],
                                       narrow[:, pos.xt[u] % 2, :]).then_inc(narrow_free, 1)
                    for u in units(prev, AT_STACK3, step):
                        copy_stack(3, pos, u)
                    for u in units(cur, AT_QEXP, step):
                        query_exp(pos, f, u)
                    if ahead and step == AT_SQUARE1:
                        square(1, m)
                    if prev and step == AT_ROUTER:
                        act.wait_ge(small_full, pos.s + pos.logit + 1)
                        nc.scalar.copy(logit[:].rearrange("p g e -> p (g e)"),
                                       small[:, 0:G * E]).then_inc(small_free, 1)
                    if prev and step == AT_RESIDUAL:
                        act.wait_ge(x2_ready, g + 1)
                        if not (isinstance(g, int) and g == 0):
                            act.wait_ge(out_full, OUTU * g)
                        nc.scalar.copy(residual[:], x2[:]).then_inc(residual_ready, 1)
                    if prev and step == AT_E2:
                        act.wait_ge(gap_ready, g + 1)
                        nc.scalar.activation(e2[:], gap[:], ACT.Exp, scale=wscale[:, 2:3]).then_inc(e2_ready, 1)
                    if nxt and step == AT_SPLIT1:
                        high_parts(1, n, xhat[:, :, 0:C])
                    for u in units(nxt, AT_STACK1, step):
                        copy_stack(1, pos, u)
                    if cur and step == AT_SQUARE2:
                        square(2, f)
                    if cur and step == AT_SQUARE3:
                        square(3, f)
                    for u in units(nxt, AT_KEXP, step):
                        key_exp(pos, n, u)
                    for half in units(nxt, AT_QROWS, step):
                        act.wait_ge(narrow_full, pos.n + pos.qrows[half] + 1)
                        nc.scalar.copy(qmax_tr[:, half, :],
                                       narrow[:, pos.qrows[half] % 2, 0:P // 2].bitcast(f16)).then_inc(narrow_free, 1)
                    if prev and step in AT_OUT[3::4]:
                        copy_output(g, AT_OUT.index(step) // 4)
                    if cur and step == AT_SPLIT3:
                        high_parts(3, f, xhat3[:])

            run(act, iteration, set_up)

        @block.vector
        def _(dve):
            def set_up():
                st = Chain(dve, setup_v, 0)
                dve.wait_ge(loaded, 16 * 15)
                dve.wait_ge(made, 20)
                for r in range(3):
                    st.inc(nc.vector.tensor_copy(qk_nat[:, :, C * r:C * r + C], w_nat[:, 0:2, :]))
                for r in (96, 97):
                    st.inc(nc.vector.tensor_copy(qk_nat[:, :, r:r + 1], b_nat[:, 0:2].unsqueeze(2)))
                st.inc(nc.vector.tensor_copy(v_nat[:, 0:C], w_nat[:, 2, :]))
                st.inc(nc.vector.tensor_copy(v_nat[:, C:C + 1], b_nat[:, 2:3]))
                st.inc(nc.vector.tensor_scalar(ctxscale[:], headmask[:], SCALE / N, None, ALU.mult))
                st.inc(nc.vector.tensor_reduce(bout_mean[:], bout_rep[:], AX.X, ALU.add, negate=True))
                st.wait()
                st.inc(nc.vector.tensor_scalar(bout_mean[:], bout_mean[:], 1.0 / C, None, ALU.mult))
                st.wait()
                st.inc(nc.vector.tensor_scalar(bout_centered[:], bout_rep[:], bout_mean[:], None, ALU.add))
                st.wait()
                st.inc(nc.vector.scalar_tensor_tensor(ctxbias[:], headmask[:], 1.0 / HEADS,
                                                      bout_centered[:].unsqueeze(1).broadcast_to([P, HEADS, C]),
                                                      ALU.mult, ALU.mult))
                st.inc(nc.vector.tensor_copy(mixz[:, P:P + HEADS], headmask[:, :, 0]))
                st.inc(nc.vector.tensor_copy(u_mat[:, P:P + 1], ident[0:C + 1, C:C + 1]))
                dve.wait_ge(setup_t, 1)
                st.inc(nc.vector.tensor_copy(w_rows[:, 0:2 * CH], wide[:, 0, 0:2 * CH]))
                st.inc(nc.vector.tensor_tensor(wo_block[:], headmask[:],
                                               wide[:, 0, 256:256 + C].unsqueeze(1).broadcast_to([P, HEADS, C]),
                                               ALU.mult))
                st.wait()
                for n, (lo, hi) in enumerate(groups):
                    st.inc(nc.vector.tensor_reduce(amax[:, n:n + 1], w_rows[:, lo:hi], AX.X, ALU.max,
                                                   apply_absolute_value=True))
                dve.wait_ge(setup_t, 2)
                st.inc(nc.vector.tensor_reduce(gmax[:], wide[0:3, 1, 0:P], AX.X, ALU.max))
                u_psum = wide[0:C + 1, 1, 512:512 + P].rearrange("p (h o) -> p h o", h=HEADS)
                st.inc(nc.vector.tensor_reduce(u_mean[:], u_psum, AX.X, ALU.add, negate=True))
                st.wait()
                st.inc(nc.vector.tensor_scalar(u_mean[:], u_mean[:], 1.0 / C, None, ALU.mult))
                st.wait()
                st.inc(nc.vector.tensor_tensor(u_mat[:, 0:P].rearrange("p (h o) -> p h o", h=HEADS), u_psum,
                                               u_mean[:].unsqueeze(2).broadcast_to([C + 1, HEADS, C]), ALU.add))
                st.inc(nc.vector.tensor_scalar(gmax[:], gmax[:], 1e-30, None, ALU.max))
                st.wait()
                st.inc(nc.vector.tensor_scalar(gpow[:].bitcast(u32), gmax[:].bitcast(u32), 0x7F800000, None,
                                               ALU.bitwise_and))
                st.wait()
                st.inc(nc.vector.tensor_scalar(gdiag[:], ident[0:3, 0:3], gpow[:], None, ALU.mult))
                dve.wait_ge(setup_t, 3)
                st.inc(nc.vector.tensor_copy(wscale[:], wide[:, 0, 0:3]))
                st.wait()
                st.inc(nc.vector.reciprocal(winv[:], wscale[:]))
                st.wait()
                for n, (lo, hi) in enumerate(groups):
                    st.inc(nc.vector.tensor_scalar(w_rows[:, lo:hi], w_rows[:, lo:hi], winv[:, n:n + 1], None,
                                                   ALU.mult))
                st.wait()
                st.inc(nc.vector.tensor_copy(w_high[:], w_rows[:]))
                st.wait()
                st.inc(nc.vector.tensor_tensor(w_low[:], w_rows[:], w_high[:], ALU.subtract))
                st.wait()
                st.inc(nc.vector.tensor_scalar(w_high[:], w_high[:], row_high[:], None, ALU.mult))
                st.wait()
                st.inc(nc.vector.scalar_tensor_tensor(w_stack[:], w_low[:], row_low[:], w_high[:], ALU.mult, ALU.add))
                st.wait()
                assert st.n == SETUP_V, st.n

            def tiles(flat):
                return flat.rearrange("p (g c) -> p g c", c=C)

            def over_experts(stat):
                return stat[:].unsqueeze(2).broadcast_to([P, G, E])

            def mean(k, c, src):
                c.inc(nc.vector.tensor_reduce(nsum[k][:], tiles(src), AX.X, ALU.add, negate=True))
                c.wait()
                nc.vector.tensor_scalar(nmean[k][:], nsum[k][:], 1.0 / C, None, ALU.mult).then_inc(mean_ready[k], 1)

            def inverse_root(k, c, b, eps, part):
                if part == 0:
                    dve.wait_ge(square_ready[k], b + 1)
                    c.inc(nc.vector.tensor_reduce(vsum[k][:], tiles(squares[k][:]), AX.X, ALU.add))
                elif part == 1:
                    c.wait()
                    c.inc(nc.vector.tensor_scalar(vari[k][:], vsum[k][:], 1.0 / C, eps, ALU.mult, ALU.add))
                    c.wait()
                    c.inc(nc.vector.tensor_scalar(root[k][:].bitcast(i32), vari[k][:].bitcast(i32), -0.5,
                                                  float(0x5F1FFFF9), ALU.mult, ALU.add))
                    c.wait()
                    c.inc(nc.vector.tensor_tensor(rr[k][:], root[k][:], root[k][:], ALU.mult))
                elif part == 2:
                    c.wait()
                    c.inc(nc.vector.scalar_tensor_tensor(ru[k][:], rr[k][:], -0.375 * 0.703952253, vari[k][:],
                                                         ALU.mult, ALU.mult))
                    c.wait()
                    c.inc(nc.vector.scalar_tensor_tensor(root[k][:], ru[k][:], 0.375 * 0.703952253 * 2.38924456,
                                                         root[k][:], ALU.add, ALU.mult))
                    c.wait()
                    c.inc(nc.vector.tensor_tensor(rr[k][:], root[k][:], root[k][:], ALU.mult))
                else:
                    c.wait()
                    c.inc(nc.vector.scalar_tensor_tensor(ru[k][:], rr[k][:], 64.0 / 9.0, vari[k][:],
                                                         ALU.mult, ALU.mult))
                    c.wait()
                    c.inc(nc.vector.scalar_tensor_tensor(rr[k][:], ru[k][:], -10.0 / 3.0, ru[k][:],
                                                         ALU.add, ALU.mult))
                    c.wait()
                    nc.vector.scalar_tensor_tensor(rstd[k][:], rr[k][:], 5.0, root[k][:], ALU.add,
                                                   ALU.mult).then_inc(rstd_ready[k], 1)

            def low_part(k, b, src):
                dve.wait_ge(high_ready[k], b + 1)
                nc.vector.tensor_tensor(parts[k][:, :, C:2 * C], src, parts[k][:, :, 0:C],
                                        ALU.subtract).then_inc(parts_ready[k], 1)

            def query_max(pos, c, u):
                half = u // 2
                dve.wait_ge(wide_full, pos.w + pos.qmax[u] + 1)
                nc.vector.tensor_reduce(nqmax[:, half, 32 * (u % 2):32 * (u % 2) + 32],
                                        wide[:, pos.qmax[u] % 2, :].rearrange("p (a d) -> p a d", d=DH),
                                        AX.X, ALU.max, negate=True).then_inc(wide_free, 1)
                if u % 2:
                    dve.wait_ge(wide_free, pos.w + pos.qmax[u] + 1)
                    c.inc(nc.vector.tensor_copy(qmax_nat[:, half, 0, :], nqmax[:, half, :]))
                    c.wait()
                    nc.vector.tensor_tensor(qmax_nat[:, half, 1, :], nqmax[:, half, :], qmax_nat[:, half, 0, :],
                                            ALU.subtract).then_inc(qmax_nat_ready, 1)

            def normalise(pos, c, u):
                dve.wait_ge(wide_full, pos.w + pos.norm[u] + 1)
                src = wide[:, pos.norm[u] % 2, :].rearrange("p (t c) -> p t c", t=4)
                c.inc(nc.vector.reciprocal(zrec[:, u % 2, :, :], src[:, :, P:P + HEADS]))
                c.wait()
                nc.vector.tensor_tensor(
                    heads[:, 4 * u:4 * u + 4, :].rearrange("p t (h c) -> p t h c", h=HEADS),
                    src[:, :, 0:P].rearrange("p t (h c) -> p t h c", h=HEADS),
                    zrec[:, u % 2, :, :].unsqueeze(3).broadcast_to([P, 4, HEADS, C]),
                    ALU.mult).then_inc(wide_free, 1)

            def key_max(pos, u):
                dve.wait_ge(wide_full, pos.w + pos.kmax[u] + 1)
                nc.vector.tensor_reduce(kmax[:, u:u + 1], wide[:, pos.kmax[u] % 2, :], AX.X,
                                        ALU.max).then_inc(wide_free, 1)

            def key_max_parts(pos, c):
                dve.wait_ge(wide_free, pos.w + pos.kmax[KMAX - 1] + 1)
                c.inc(nc.vector.tensor_reduce(nkmax[:], kmax[:], AX.X, ALU.max, negate=True))
                c.wait()
                c.inc(nc.vector.tensor_copy(kmax_nat[:, 98:99], nkmax[:]))
                c.wait()
                nc.vector.tensor_tensor(kmax_nat[:, 99:100], nkmax[:], kmax_nat[:, 98:99],
                                        ALU.subtract).then_inc(kmax_nat_ready, 1)

            def weights_with_key_max(pos):
                dve.wait_ge(small_full, pos.s + pos.ktr + 1)
                nc.vector.tensor_tensor(ws_kmax[:], ws_k, small[:, 0:P // 2].bitcast(f16),
                                        ALU.add).then_inc(small_free, 1)

            def context(pos, c, n, part):
                if part == 0:
                    dve.wait_ge(small_full, pos.s + pos.ctx + 1)
                    nc.vector.tensor_copy(sums_ctx[:], small[0:C + 1, 0:P]).then_inc(small_free, 1)
                else:
                    dve.wait_ge(small_full, pos.s + pos.mix + 1)
                    c.inc(nc.vector.reciprocal(grec[:], small[:, P:P + 1]))
                    c.wait()
                    nc.vector.scalar_tensor_tensor(mix[:], small[:, 0:P], grec[:],
                                                   ctxscale[:].rearrange("p h c -> p (h c)"),
                                                   ALU.mult, ALU.mult).then_inc(small_free, 1)
                    dve.wait_ge(small_free, pos.s + pos.mix + 1)
                    nc.vector.tensor_tensor(mixz[:, 0:P], mix[:], ctxbias[:].rearrange("p h c -> p (h c)"),
                                            ALU.add).then_inc(mixz_ready, 1)

            def route(pos, c, g, part):
                def step(ins):
                    c.inc(ins)
                    c.wait()

                if part == 0:
                    dve.wait_ge(small_free, pos.s + pos.logit + 1)
                    step(nc.vector.tensor_reduce(top1[:], logit[:], AX.X, ALU.max))
                    step(nc.vector.tensor_tensor(tie1[:], logit[:], over_experts(top1), ALU.is_equal))
                elif part == 1:
                    step(nc.vector.tensor_tensor(tie1[:], tie1[:], rank[:], ALU.mult))
                    step(nc.vector.tensor_reduce(pick1[:], tie1[:], AX.X, ALU.max))
                elif part == 2:
                    step(nc.vector.tensor_tensor(one1[:], tie1[:], over_experts(pick1), ALU.is_equal))
                    step(nc.vector.scalar_tensor_tensor(logit2[:].rearrange("p g e -> p (g e)"),
                                                        one1[:].rearrange("p g e -> p (g e)"), -3.0e38,
                                                        logit[:].rearrange("p g e -> p (g e)"), ALU.mult, ALU.add))
                elif part == 3:
                    step(nc.vector.tensor_reduce(top2[:], logit2[:], AX.X, ALU.max))
                    nc.vector.tensor_tensor(gap[:], top2[:], top1[:], ALU.subtract).then_inc(gap_ready, 1)
                    step(nc.vector.tensor_tensor(tie2[:], logit2[:], over_experts(top2), ALU.is_equal))
                elif part == 4:
                    step(nc.vector.tensor_tensor(tie2[:], tie2[:], rank[:], ALU.mult))
                    step(nc.vector.tensor_reduce(pick2[:], tie2[:], AX.X, ALU.max))
                    step(nc.vector.tensor_tensor(one2[:], tie2[:], over_experts(pick2), ALU.is_equal))
                elif part == 5:
                    dve.wait_ge(e2_ready, g + 1)
                    step(nc.vector.tensor_scalar(den[:], e2[:], 1.0, None, ALU.add))
                    step(nc.vector.reciprocal(g1[:], den[:]))
                    step(nc.vector.tensor_scalar(g1[:], g1[:], wscale[:, 1:2], None, ALU.mult))
                    nc.vector.tensor_tensor(g2[:], g1[:], e2[:], ALU.mult).then_inc(probs_ready, 1)

            def gate(pos, g, u):
                dve.wait_ge(wide_full, pos.w + pos.gate[u] + 1)
                if u == 0:
                    dve.wait_ge(gates_ready, g + 1)
                if u >= GATEDS:
                    dve.wait_ge(gated_used, GATE * g + u - GATEDS + 1)
                nc.vector.tensor_tensor(
                    gated[:, u % GATEDS, :, :, :].rearrange("p e t c -> p t e c"),
                    wide[:, pos.gate[u] % 2, :].rearrange("p (t e c) -> p t e c", t=4, e=E),
                    gates[:, 4 * u:4 * u + 4, :].unsqueeze(3).broadcast_to([P, 4, E, C]),
                    ALU.mult).then_inc(wide_free, 1)

            def iteration(i, cur, prev, nxt, ahead):
                f, g, n, m, pos = i, i - 1, i + 1, i + 2, Places(i, cur, prev, nxt, ahead)
                c1, ckq, cn = Chain(dve, ln1_v, LN1_V * m), Chain(dve, kq_v, KQ_V * n), Chain(dve, norm_v, NORM * f)
                c23, cr = Chain(dve, ln23_v, LN23_V * f), Chain(dve, route_v, ROUTE_V * g)
                for step in STEPS:
                    if ahead and step == AT_MEAN1:
                        dve.wait_ge(narrow_free, pos.n + pos.xt[XT - 1] + 1)
                        mean(1, c1, x_tok[:, m % 2, :])
                    for u in units(cur, AT_ATTEND, step):
                        normalise(pos, cn, u)
                    for part in units(nxt, AT_CONTEXT, step):
                        context(pos, ckq, n, part)
                    for part in units(ahead, AT_RSTD1, step):
                        inverse_root(1, c1, m, EPS_IN, part)
                    for part in units(prev, AT_ROUTE, step):
                        route(pos, cr, g, part)
                    if nxt and step == AT_SPLIT1:
                        low_part(1, n, xhat[:, :, 0:C])
                    for u in units(prev, AT_EXPERTS, step):
                        gate(pos, g, u)
                    for u in units(nxt, AT_KMAX, step):
                        key_max(pos, u)
                    if nxt and step == AT_KROW:
                        key_max_parts(pos, ckq)
                    for u in units(nxt, AT_QMAX, step):
                        query_max(pos, ckq, u)
                    if nxt and step == AT_KROW_ADD:
                        weights_with_key_max(pos)
                    for part in units(cur, AT_RSTD2, step):
                        inverse_root(2, c23, f, EPS, part)
                    if cur and step == AT_MEAN3:
                        dve.wait_ge(x2_ready, f + 1)
                        mean(3, c23, x2[:])
                    for part in units(cur, AT_RSTD3, step):
                        inverse_root(3, c23, f, EPS, part)
                    if cur and step == AT_SPLIT3:
                        low_part(3, f, xhat3[:])
                assert not ahead or c1.n == LN1_V, c1.n
                assert not nxt or ckq.n == KQ_V, ckq.n
                assert not cur or c23.n == LN23_V, c23.n
                assert not prev or cr.n == ROUTE_V, cr.n

            run(dve, iteration, set_up)

        @block.tensor
        def _(pe):
            def mm(dst, lhs, rhs, start=True, stop=True):
                return nc.tensor.matmul(dst, lhs, rhs, start=start, stop=stop)

            def tr(dst, src, idt, start=True, stop=True):
                return nc.tensor.matmul(dst, src, idt, is_transpose=True, start=start, stop=stop)

            pe.wait_ge(made, 10)

            def set_up():
                pe.wait_ge(setup_v, 7)
                for s in range(2):
                    tr(wide[:, 0, P * s:P * s + P], qk_nat[:, s, :], ident[:])
                tr(wide[:, 0, 256:256 + C], wo_nat[:, :], ident[0:C, 0:C]).then_inc(setup_t, 1)
                pe.wait_ge(setup_v, 19)
                tr(wide[0:3, 1, 0:P], amax[:, :], ident[:])
                mm(wide[0:C + 1, 1, 512:512 + P], v_nat[:, :],
                   wo_block[:].rearrange("p h c -> p (h c)")).then_inc(setup_t, 1)
                pe.wait_ge(setup_v, 26)
                mm(wide[:, 0, 0:3], ones[0:3, :], gdiag[:, :]).then_inc(setup_t, 1)
                pe.wait_ge(setup_v, SETUP_V)

            def to_tokens(pos, m, u):
                if u == 0:
                    pe.wait_ge(x_loaded, 16 * m + 16)
                wait_slot(pe, narrow_free, pos.n + pos.xt[u], 2)
                for t in range(4):
                    ins = tr(narrow[:, pos.xt[u] % 2, P * t:P * t + P],
                             x_in[:, 512 * u + P * t:512 * u + P * t + P], ident[:])
                ins.then_inc(narrow_full, 1)

            def query_logits_by_token(pos, u):
                pe.wait_ge(narrow_free, pos.n + pos.stack[1][u] + 1)
                wait_slot(pe, wide_free, pos.w + pos.qmax[u], 2)
                for t in range(8):
                    tile = P * (8 * u + t)
                    ins = mm(wide[:, pos.qmax[u] % 2, P * t:P * t + P], stack[1][:, tile:tile + P], ws_q)
                ins.then_inc(wide_full, 1)

            def query_max_rows(pos, n, half):
                pe.wait_ge(qmax_nat_ready, 2 * n + half + 1)
                wait_slot(pe, narrow_free, pos.n + pos.qrows[half], 2)
                tr(narrow[:, pos.qrows[half] % 2, 0:P // 2].bitcast(f16),
                   qmax_nat[:, half, :, :].rearrange("p a b -> p (a b)"), ident16[:]).then_inc(narrow_full, 1)

            def attend(pos, u):
                pe.wait_ge(narrow_free, pos.n + pos.qexp[u] + 1)
                wait_slot(pe, wide_free, pos.w + pos.norm[u], 2)
                for t in range(4):
                    ins = mm(wide[:, pos.norm[u] % 2, 256 * t:256 * t + P + HEADS],
                             eq[:, u % EQS, P * t:P * t + P], mixz[:, :])
                ins.then_inc(wide_full, 1)

            def query_logits(pos, u):
                half = u // 4
                if u == 0:
                    pe.wait_ge(narrow_free, pos.n)
                wait_slot(pe, narrow_free, pos.n + pos.qexp[u], 2)
                slot = pos.qexp[u] % 2
                mm(narrow[:, slot, :], ws_q, stack[1][:, 512 * u:512 * u + 512], stop=False)
                for t in range(4):
                    ins = mm(narrow[:, slot, P * t:P * t + P], maxpick[:, 4 * (u % 4) + t, :],
                             qmax_tr[:, half, :], start=False, stop=(t == 3))
                ins.then_inc(narrow_full, 1)

            def make_stack(k, pos, b, u):
                if u == 0:
                    pe.wait_ge(parts_ready[k], 2 * b + 2)
                wait_slot(pe, narrow_free, pos.n + pos.stack[k][u], 2)
                for t in range(8):
                    ins = tr(narrow[:, pos.stack[k][u] % 2, P // 2 * t:P // 2 * t + P // 2].bitcast(f16),
                             parts[k][:, 8 * u + t, :], ident16[:])
                ins.then_inc(narrow_full, 1)

            def key_logits_by_channel(pos, u):
                pe.wait_ge(narrow_free, pos.n + pos.stack[1][u] + 1)
                wait_slot(pe, wide_free, pos.w + pos.kmax[u], 2)
                for h in range(2):
                    at = 1024 * u + 512 * h
                    ins = mm(wide[:, pos.kmax[u] % 2, 512 * h:512 * h + 512], ws_k, stack[1][:, at:at + 512])
                ins.then_inc(wide_full, 1)

            def key_logits_by_token(pos, u):
                if u == 0:
                    pe.wait_ge(small_free, pos.s + pos.ktr + 1)
                wait_slot(pe, narrow_free, pos.n + pos.kexp[u], 2)
                for t in range(4):
                    tile = P * (4 * u + t)
                    ins = mm(narrow[:, pos.kexp[u] % 2, P * t:P * t + P], stack[1][:, tile:tile + P], ws_kmax[:])
                ins.then_inc(narrow_full, 1)

            def sum_context(pos, n, u):
                pe.wait_ge(narrow_free, pos.n + pos.kexp[u] + 1)
                if u == 0:
                    wait_slot(pe, small_free, pos.s + pos.ctx, 1)
                for t in range(4):
                    ins = mm(small[0:C + 1, 0:P], xhat[:, 4 * u + t, :], ek[:, u % EKS, t, :],
                             start=(u == 0 and t == 0), stop=(u == KEXP - 1 and t == 3))
                ins.then_inc(ek_used, 1)
                if u == KEXP - 1:
                    pe.wait_ge(ek_used, KEXP * n + KEXP)
                    pe.sem_inc(small_full, 1)

            def key_max_row(pos, f):
                pe.wait_ge(kmax_nat_ready, f + 1)
                wait_slot(pe, small_free, pos.s + pos.ktr, 1)
                tr(small[:, 0:P // 2].bitcast(f16), kmax_nat[:, :], ident16[:]).then_inc(small_full, 1)

            def mix_context(pos):
                pe.wait_ge(small_free, pos.s + pos.ctx + 1)
                mm(small[:, 0:P + 1], sums_ctx[:, :], u_mat[:, :]).then_inc(small_full, 1)

            def router(pos):
                pe.wait_ge(narrow_free, pos.n + pos.stack[3][STACK - 1] + 1)
                wait_slot(pe, small_free, pos.s + pos.logit, 1)
                for t in range(G):
                    ins = mm(small[:, E * t:E * t + E], stack[3][:, P * t:P * t + P], ws_r)
                ins.then_inc(small_full, 1)

            def experts(pos, u):
                wait_slot(pe, wide_free, pos.w + pos.gate[u], 2)
                for t in range(4):
                    tile = P * (4 * u + t)
                    ins = mm(wide[:, pos.gate[u] % 2, 256 * t:256 * t + 256], stack[3][:, tile:tile + P], ws_e)
                ins.then_inc(wide_full, 1)

            def add_experts(pos, g, v):
                pe.wait_ge(wide_free, pos.w + pos.gate[v] + 1)
                if v == 0:
                    pe.wait_ge(residual_ready, g + 1)
                if v % 4 == 0:
                    if not (isinstance(g, int) and g == 0 and v == 0):
                        pe.wait_ge(y_ready, OUTU * g + v // 4)
                dst = sums[:, P * (v % 4):P * (v % 4) + P]
                for e in range(E):
                    ins = tr(dst, gated[:, v % GATEDS, e, :, :].rearrange("p t c -> p (t c)"), ident[:],
                             start=(e == 0), stop=False)
                ins.then_inc(gated_used, 1)
                ins = tr(dst, residual[:, P * v:P * v + P], ident[:], start=False, stop=True)
                if v % 4 == 3:
                    ins.then_inc(out_full, 1)

            def iteration(i, cur, prev, nxt, ahead):
                f, g, n, m, pos = i, i - 1, i + 1, i + 2, Places(i, cur, prev, nxt, ahead)
                for step in STEPS:
                    for u in units(ahead, AT_XT, step):
                        to_tokens(pos, m, u)
                    for u in units(prev, AT_STACK3, step):
                        make_stack(3, pos, g, u)
                    for u in units(cur, AT_QEXP, step):
                        query_logits(pos, u)
                    for u in units(nxt, AT_STACK1, step):
                        make_stack(1, pos, n, u)
                    if prev and step == AT_ROUTER:
                        router(pos)
                    for u in units(nxt, AT_KEXP, step):
                        key_logits_by_token(pos, u)
                    for half in units(nxt, AT_QROWS, step):
                        query_max_rows(pos, n, half)
                    for u in units(cur, AT_ATTEND, step):
                        if u == 0:
                            pe.wait_ge(mixz_ready, f + 1)
                        attend(pos, u)
                    for u in units(prev, AT_EXPERTS, step):
                        experts(pos, u)
                    for u in units(nxt, AT_KMAX, step):
                        key_logits_by_channel(pos, u)
                    if nxt and step == AT_KROW_TURN:
                        key_max_row(pos, n)
                    for u in units(nxt, AT_QMAX, step):
                        query_logits_by_token(pos, u)
                    for u in units(prev, AT_OUT, step):
                        add_experts(pos, g, u)
                    for u in units(nxt, AT_SUMS, step):
                        sum_context(pos, n, u)
                    if nxt and step == AT_MIX:
                        mix_context(pos)

            run(pe, iteration, set_up)


_INS = ['x', 'L0_conv_w_qkv', 'L0_conv_b_qkv', 'L0_conv_w_out', 'L0_conv_b_out', 'L0_conv_g_ln',
        'L0_ffn_router_w', 'L0_ffn_router_b', 'L0_ffn_expert_w', 'L0_ffn_expert_b']


def kernel(**inputs):
    import numpy as _np
    import concourse.bacc as _bacc
    from concourse import mybir as _mybir
    from concourse.bass_utils import run_bass_kernel_spmd as _run
    nc = _bacc.Bacc("TRN2", target_bir_lowering=False, num_devices=1)
    arrays, args = {}, []
    for name in _INS:
        a = _np.ascontiguousarray(inputs[name])
        arrays[f"in_{name}_dram"] = a
        args.append(nc.dram_tensor(f"in_{name}_dram", a.shape, _mybir.dt.from_np(a.dtype), kind="ExternalInput").ap())
    out = nc.dram_tensor("out_dram", (8, 32, 64, 64), _mybir.dt.float32, kind="ExternalOutput").ap()
    build(nc, *args, out)
    r = _run(nc, [arrays], core_ids=[0])
    return r.results[0]["out_dram"]
```
